# Optimizing a Trainium2 kernel written in Bass

```python
import numpy as np
import jax
import jax.numpy as jnp

def _softmax(x, axis=-1):
    return jax.nn.softmax(x, axis=axis)

def _gelu(x):
    return jax.nn.gelu(x, approximate=True)

def _silu(x):
    return jax.nn.silu(x)

def _sigmoid(x):
    return jax.nn.sigmoid(x)

def _layernorm(x, axis=-1, eps=1e-05):
    m = jnp.mean(x, axis=axis, keepdims=True)
    v = jnp.var(x, axis=axis, keepdims=True)
    return (x - m) / jnp.sqrt(v + eps)

def _scatter_add(tgt, idx, src, axis=0):
    return tgt.at[idx].add(src)

def _segment_sum(src, seg, n):
    return jax.ops.segment_sum(src, seg, n)
kernel_name = 'mk_hybrid_d1_jaxref_r4_93db1f'

def setup_inputs(seed: int=0):
    np.random.seed(seed)
    _w = jnp.asarray

    def _L0_attn_a_setup():
        import jax, jax.numpy as jnp
        import numpy as np

        def _mamba_fwd(hidden_states, in_proj_w, conv_w, conv_b, x_proj_w, dt_proj_w, dt_proj_b, A_log, D_param, out_proj_w):
            Bsz, L, _ = hidden_states.shape
            d_inner = conv_w.shape[0]
            n = A_log.shape[1]
            r = dt_proj_w.shape[1]
            xz = jnp.einsum('bld,ed->ble', hidden_states, in_proj_w)
            x, z = (xz[..., :d_inner], xz[..., d_inner:])
            x_bdl = jnp.transpose(x, (0, 2, 1))
            kern = conv_w[:, None, :]
            xc = jax.lax.conv_general_dilated(x_bdl, kern, window_strides=(1,), padding=[(conv_w.shape[1] - 1, 0)], dimension_numbers=('NCH', 'OIH', 'NCH'), feature_group_count=d_inner)
            xc = xc + conv_b[None, :, None]
            xc = xc * jax.nn.sigmoid(xc)
            u = jnp.transpose(xc, (0, 2, 1))
            x_dbl = jnp.einsum('bld,ed->ble', u, x_proj_w)
            dt_lo = x_dbl[..., :r]
            B_ssm = x_dbl[..., r:r + n]
            C_ssm = x_dbl[..., r + n:]
            delta = jax.nn.softplus(jnp.einsum('blr,dr->bld', dt_lo, dt_proj_w) + dt_proj_b)
            A = -jnp.exp(A_log)

            def step(h, inp):
                d_t, u_t, b_t, c_t = inp
                dA = jnp.exp(d_t[..., None] * A)
                h = dA * h + (d_t * u_t)[..., None] * b_t[:, None, :]
                y_t = jnp.einsum('bdn,bn->bd', h, c_t)
                return (h, y_t)
            h0 = jnp.zeros((Bsz, d_inner, n), dtype=u.dtype)
            xs = (jnp.transpose(delta, (1, 0, 2)), jnp.transpose(u, (1, 0, 2)), jnp.transpose(B_ssm, (1, 0, 2)), jnp.transpose(C_ssm, (1, 0, 2)))
            _, ys = jax.lax.scan(step, h0, xs)
            y = jnp.transpose(ys, (1, 0, 2)) + u * D_param
            y = y * (z * jax.nn.sigmoid(z))
            return jnp.einsum('bld,ed->ble', y, out_proj_w)
        key = jax.random.key(seed)
        ks = jax.random.split(key, 10)
        B, L, D_MODEL = (2, 512, 256)
        D_INNER, N, W, R = (512, 16, 4, 64)
        s = 0.02
        return {'hidden_states': jax.random.normal(ks[0], (B, L, D_MODEL), jnp.float32), 'in_proj_w': jax.random.normal(ks[1], (2 * D_INNER, D_MODEL), jnp.float32) * s, 'conv_w': jax.random.normal(ks[2], (D_INNER, W), jnp.float32) * 0.2, 'conv_b': jax.random.normal(ks[3], (D_INNER,), jnp.float32) * 0.02, 'x_proj_w': jax.random.normal(ks[4], (R + 2 * N, D_INNER), jnp.float32) * s, 'dt_proj_w': jax.random.normal(ks[5], (D_INNER, R), jnp.float32) * R ** (-0.5), 'dt_proj_b': jnp.log(jnp.expm1(jnp.exp(jax.random.uniform(ks[6], (D_INNER,), jnp.float32, np.log(0.001), np.log(0.1)))) + 1e-20), 'A_log': jnp.log(jnp.broadcast_to(jnp.arange(1, N + 1, dtype=jnp.float32), (D_INNER, N))), 'D_param': jnp.ones((D_INNER,), jnp.float32), 'out_proj_w': jax.random.normal(ks[7], (D_MODEL, D_INNER), jnp.float32) * s}
    _L0_attn_a_in = _L0_attn_a_setup()

    def _L0_attn_b_setup():
        import jax, jax.numpy as jnp
        import numpy as np
        NUM_HEADS = 16
        EPS = 1e-06
        CHUNK = 128
        key = jax.random.key(seed)
        ks = jax.random.split(key, 6)
        B, T, E = (4, 512, 256)
        s = 0.02
        x = jax.random.normal(ks[0], (B, T, E), jnp.float32)
        Wq = jax.random.normal(ks[1], (E, E), jnp.float32) * s
        Wk = jax.random.normal(ks[2], (E, E), jnp.float32) * s
        Wv = jax.random.normal(ks[3], (E, E), jnp.float32) * s
        Wp = jax.random.normal(ks[4], (E, E), jnp.float32) * s
        bp = jnp.zeros((E,), jnp.float32)
        return {'x': x, 'Wq': Wq, 'Wk': Wk, 'Wv': Wv, 'Wp': Wp, 'bp': bp}
    _L0_attn_b_in = _L0_attn_b_setup()

    def _L0_ffn_setup():
        import jax, jax.numpy as jnp
        import numpy as np
        B, T, C, H, E = (4, 512, 256, 512, 8)
        CAPACITY_FACTOR = 1.0
        key = jax.random.key(seed)
        ks = jax.random.split(key, 5)
        scale = 0.02
        return {'x': jax.random.normal(ks[0], (B, T, C), dtype=jnp.float32), 'Wg': jax.random.normal(ks[1], (E, C), dtype=jnp.float32) * scale, 'W1': jax.random.normal(ks[2], (E, H, C), dtype=jnp.float32) * scale, 'W2': jax.random.normal(ks[3], (E, C, H), dtype=jnp.float32) * scale, 'W3': jax.random.normal(ks[4], (E, H, C), dtype=jnp.float32) * scale}
    _L0_ffn_in = _L0_ffn_setup()
    _d = {'L0_attn_a_hidden_states': _L0_attn_a_in['hidden_states'], 'L0_attn_a_in_proj_w': _L0_attn_a_in['in_proj_w'], 'L0_attn_a_conv_w': _L0_attn_a_in['conv_w'], 'L0_attn_a_conv_b': _L0_attn_a_in['conv_b'], 'L0_attn_a_x_proj_w': _L0_attn_a_in['x_proj_w'], 'L0_attn_a_dt_proj_w': _L0_attn_a_in['dt_proj_w'], 'L0_attn_a_dt_proj_b': _L0_attn_a_in['dt_proj_b'], 'L0_attn_a_A_log': _L0_attn_a_in['A_log'], 'L0_attn_a_D_param': _L0_attn_a_in['D_param'], 'L0_attn_a_out_proj_w': _L0_attn_a_in['out_proj_w'], 'L0_attn_b_Wq': _L0_attn_b_in['Wq'], 'L0_attn_b_Wk': _L0_attn_b_in['Wk'], 'L0_attn_b_Wv': _L0_attn_b_in['Wv'], 'L0_attn_b_Wp': _L0_attn_b_in['Wp'], 'L0_attn_b_bp': _L0_attn_b_in['bp'], 'L0_ffn_Wg': _L0_ffn_in['Wg'], 'L0_ffn_W1': _L0_ffn_in['W1'], 'L0_ffn_W2': _L0_ffn_in['W2'], 'L0_ffn_W3': _L0_ffn_in['W3']}
    _x0 = _d['L0_attn_a_hidden_states']
    _d['L0_attn_a_hidden_states'] = jax.random.normal(jax.random.fold_in(jax.random.key(seed), 1), (16, 512, 256), dtype=_x0.dtype)
    del _x0
    return _d

def reference(L0_attn_a_hidden_states, L0_attn_a_in_proj_w, L0_attn_a_conv_w, L0_attn_a_conv_b, L0_attn_a_x_proj_w, L0_attn_a_dt_proj_w, L0_attn_a_dt_proj_b, L0_attn_a_A_log, L0_attn_a_D_param, L0_attn_a_out_proj_w, L0_attn_b_Wq, L0_attn_b_Wk, L0_attn_b_Wv, L0_attn_b_Wp, L0_attn_b_bp, L0_ffn_Wg, L0_ffn_W1, L0_ffn_W2, L0_ffn_W3):

    def _L0_attn_a_ref(hidden_states, in_proj_w, conv_w, conv_b, x_proj_w, dt_proj_w, dt_proj_b, A_log, D_param, out_proj_w):
        import jax, jax.numpy as jnp
        import numpy as np

        def _mamba_fwd(hidden_states, in_proj_w, conv_w, conv_b, x_proj_w, dt_proj_w, dt_proj_b, A_log, D_param, out_proj_w):
            Bsz, L, _ = hidden_states.shape
            d_inner = conv_w.shape[0]
            n = A_log.shape[1]
            r = dt_proj_w.shape[1]
            xz = jnp.einsum('bld,ed->ble', hidden_states, in_proj_w)
            x, z = (xz[..., :d_inner], xz[..., d_inner:])
            x_bdl = jnp.transpose(x, (0, 2, 1))
            kern = conv_w[:, None, :]
            xc = jax.lax.conv_general_dilated(x_bdl, kern, window_strides=(1,), padding=[(conv_w.shape[1] - 1, 0)], dimension_numbers=('NCH', 'OIH', 'NCH'), feature_group_count=d_inner)
            xc = xc + conv_b[None, :, None]
            xc = xc * jax.nn.sigmoid(xc)
            u = jnp.transpose(xc, (0, 2, 1))
            x_dbl = jnp.einsum('bld,ed->ble', u, x_proj_w)
            dt_lo = x_dbl[..., :r]
            B_ssm = x_dbl[..., r:r + n]
            C_ssm = x_dbl[..., r + n:]
            delta = jax.nn.softplus(jnp.einsum('blr,dr->bld', dt_lo, dt_proj_w) + dt_proj_b)
            A = -jnp.exp(A_log)

            def step(h, inp):
                d_t, u_t, b_t, c_t = inp
                dA = jnp.exp(d_t[..., None] * A)
                h = dA * h + (d_t * u_t)[..., None] * b_t[:, None, :]
                y_t = jnp.einsum('bdn,bn->bd', h, c_t)
                return (h, y_t)
            h0 = jnp.zeros((Bsz, d_inner, n), dtype=u.dtype)
            xs = (jnp.transpose(delta, (1, 0, 2)), jnp.transpose(u, (1, 0, 2)), jnp.transpose(B_ssm, (1, 0, 2)), jnp.transpose(C_ssm, (1, 0, 2)))
            _, ys = jax.lax.scan(step, h0, xs)
            y = jnp.transpose(ys, (1, 0, 2)) + u * D_param
            y = y * (z * jax.nn.sigmoid(z))
            return jnp.einsum('bld,ed->ble', y, out_proj_w)
        return _mamba_fwd(hidden_states, in_proj_w, conv_w, conv_b, x_proj_w, dt_proj_w, dt_proj_b, A_log, D_param, out_proj_w)

    def _L0_attn_b_ref(x, Wq, Wk, Wv, Wp, bp):
        import jax, jax.numpy as jnp
        import numpy as np
        NUM_HEADS = 16
        EPS = 1e-06
        CHUNK = 128
        B, T, E = x.shape
        H = NUM_HEADS
        D = E // H
        N = T // CHUNK
        q = x @ Wq.T
        k = x @ Wk.T
        v = x @ Wv.T

        def split_heads(t):
            return t.reshape(B, T, H, D).transpose(0, 2, 1, 3).reshape(B, H, N, CHUNK, D)
        phi_q = jax.nn.elu(split_heads(q)) + 1.0
        phi_k = jax.nn.elu(split_heads(k)) + 1.0
        vh = split_heads(v)
        kv = jnp.einsum('bhncd,bhnce->bhnde', phi_k, vh)
        zk = phi_k.sum(axis=3)
        S_prev = jnp.concatenate([jnp.zeros_like(kv[:, :, :1]), jnp.cumsum(kv, axis=2)[:, :, :-1]], axis=2)
        Z_prev = jnp.concatenate([jnp.zeros_like(zk[:, :, :1]), jnp.cumsum(zk, axis=2)[:, :, :-1]], axis=2)
        A = jnp.einsum('bhncd,bhnsd->bhncs', phi_q, phi_k)
        mask = jnp.tril(jnp.ones((CHUNK, CHUNK), bool))
        A = jnp.where(mask, A, 0.0)
        num = jnp.einsum('bhncs,bhnse->bhnce', A, vh) + jnp.einsum('bhncd,bhnde->bhnce', phi_q, S_prev)
        den = A.sum(-1) + jnp.einsum('bhncd,bhnd->bhnc', phi_q, Z_prev) + EPS
        y = num / den[..., None]
        y = y.reshape(B, H, T, D).transpose(0, 2, 1, 3).reshape(B, T, E)
        return y @ Wp.T + bp

    def _L0_ffn_ref(x, Wg, W1, W2, W3):
        import jax, jax.numpy as jnp
        import numpy as np
        B, T, C, H, E = (4, 512, 256, 512, 8)
        CAPACITY_FACTOR = 1.0
        b, t, c = x.shape
        e = Wg.shape[0]
        n = b * t
        capacity = max(1, int(CAPACITY_FACTOR * n / e))
        x_flat = x.reshape(n, c)
        scores = (x_flat @ Wg.T).T
        top_vals, token_idx = jax.lax.top_k(scores, capacity)
        token_w = jax.nn.softmax(top_vals, axis=-1)
        xg = x_flat[token_idx]
        h = jax.nn.silu(jnp.einsum('eic,ehc->eih', xg, W1)) * jnp.einsum('eic,ehc->eih', xg, W3)
        y = jnp.einsum('eih,ech->eic', h, W2) * token_w[..., None]
        out = jnp.zeros_like(x_flat).at[token_idx.reshape(-1)].add(y.reshape(-1, c))
        return out.reshape(b, t, c)
    x = L0_attn_a_hidden_states
    x = x + _L0_attn_a_ref(_layernorm(x, axis=-1), L0_attn_a_in_proj_w, L0_attn_a_conv_w, L0_attn_a_conv_b, L0_attn_a_x_proj_w, L0_attn_a_dt_proj_w, L0_attn_a_dt_proj_b, L0_attn_a_A_log, L0_attn_a_D_param, L0_attn_a_out_proj_w)
    x = x + _L0_ffn_ref(_layernorm(x, axis=-1), L0_ffn_Wg, L0_ffn_W1, L0_ffn_W2, L0_ffn_W3)
    x = x + _L0_attn_b_ref(_layernorm(x, axis=-1), L0_attn_b_Wq, L0_attn_b_Wk, L0_attn_b_Wv, L0_attn_b_Wp, L0_attn_b_bp)
    x = x + _L0_ffn_ref(_layernorm(x, axis=-1), L0_ffn_Wg, L0_ffn_W1, L0_ffn_W2, L0_ffn_W3)
    return x

_drawn_inputs = setup_inputs


def setup_inputs(seed=0):
    import zlib

    import numpy as np

    out = dict(_drawn_inputs(seed))
    spreads = {'L0_attn_a_D_param': (1.0, 0.2), 'L0_attn_b_bp': (0.0, 0.1)}
    factors = {}
    for name, (base, spread) in spreads.items():
        noise = np.random.default_rng([zlib.crc32(name.encode()), seed]).standard_normal(out[name].shape)
        drawn = base * np.exp(spread * noise) if base else spread * noise
        out[name] = jnp.asarray(drawn.astype(out[name].dtype))
    for name, factor in factors.items():
        out[name] = (out[name] * factor).astype(out[name].dtype)
    return out
```

```python
from contextlib import ExitStack

import concourse.bass as bass
from concourse import mybir

F32 = mybir.dt.float32
BF16 = mybir.dt.bfloat16
I32 = mybir.dt.int32
ALU = mybir.AluOpType
ACT = mybir.ActivationFunctionType
AX = mybir.AxisListType

P = 128
NB = 16
T = 512
C = 256
KC = C // P
TJ = T // P
NTOK = NB * T
EPS = 1e-5

DI = 512
KD = DI // P
NS = 16
RK = 64
CW = 4
HALO = CW - 1
UN = KD * NS

NE = 8
CAP = NTOK // NE
FH = 512
KF = FH // P
NSLOT = CAP // P


class Scope:

    def __init__(self, nc, stack, name):
        self.nc, self.stack, self.name, self.sems = nc, stack, name, []

    def sb(self, name, shape, dt=F32):
        return self.stack.enter_context(self.nc.sbuf_tensor(f"{self.name}_{name}", shape, dt))

    def ps(self, name, shape, dt=F32):
        return self.stack.enter_context(self.nc.psum_tensor(f"{self.name}_{name}", shape, dt))

    def sem(self, name):
        self.sems.append(self.stack.enter_context(self.nc.semaphore(f"{self.name}_{name}")))
        return self.sems[-1]

    def clear(self):
        with self.nc.Block() as block:
            @block.sync
            def _(sp):
                for sem in self.sems:
                    sp.sem_clear(sem)


def turns(eng, n, prologue, body, epilogue):
    prologue()
    body(0, 0, True, False)
    body(1, 1, False, False)
    with eng.Fori(1, n // 2 - 1) as k:
        for q in range(2):
            body(eng.snap(k * 2 + q), q, False, False)
    body(n - 2, 0, False, False)
    body(n - 1, 1, False, True)
    epilogue()


def mamba(nc, x, x1, xn1, scores, w):
    with ExitStack() as stack:
        s = Scope(nc, stack, "m")
        w_in = s.sb("w_in", [P, KC, 2 * DI])
        w_xd = s.sb("w_xd", [P, KD, RK])
        w_xb = s.sb("w_xb", [P, KD, 6 * NS])
        w_dt = s.sb("w_dt", [RK, DI])
        w_out = s.sb("w_out", [P, KD, C])
        w_g = s.sb("w_g", [P, KC, NE])
        conv_w = s.sb("conv_w", [P, KD, CW])
        conv_b = s.sb("conv_b", [P, KD])
        dt_b = s.sb("dt_b", [P, KD])
        d_par = s.sb("d_par", [P, KD])
        a_log = s.sb("a_log", [P, KD, NS])
        a_neg = s.sb("a_neg", [P, KD, NS])
        ident = s.sb("ident", [P, P])
        pick = s.sb("pick", [6 * NS, 2 * NS])
        pickb = s.sb("pickb", [6 * NS, 2 * NS], BF16)
        nhalf = s.sb("nhalf", [P, TJ])
        xt = s.sb("xt", [P, TJ, C])
        stat = s.sb("stat", [P, TJ, 6])
        mv = s.sb("mv", [P, TJ, 2])
        ve = s.sb("ve", [P, TJ])
        rstd = s.sb("rstd", [P, TJ])
        xn = s.sb("xn", [P, TJ, C])
        xnT = s.sb("xnT", [P, KC, T])
        xs = s.sb("xs", [P, 2, HALO + T])
        dtlo = s.sb("dtlo", [RK, T])
        bc1 = s.sb("bc1", [6 * NS, T], BF16)
        bcr = s.sb("bcr", [6 * NS, T])
        bc2 = s.sb("bc2", [6 * NS, T], BF16)
        sp = s.sb("sp", [P, 2, T])
        u = s.sb("u", [P, 2, KD, T])
        sz = s.sb("sz", [P, 2, KD, T])
        delta = s.sb("delta", [P, 2, KD, T])
        du = s.sb("du", [P, 2, KD, T])
        bc = s.sb("bc", [P, 2 * NS, T])
        dbu = s.sb("dbu", [P, 4, T])
        hc = s.sb("hc", [P, 4, T])
        yg = s.sb("yg", [P, KD, T])
        xr = s.sb("xr", [P, TJ, C])
        x1t = xr
        stat1 = s.sb("stat1", [P, TJ, 6])
        mv1 = s.sb("mv1", [P, TJ, 2])
        ve1 = s.sb("ve1", [P, TJ])
        rstd1 = s.sb("rstd1", [P, TJ])
        xn1t = s.sb("xn1t", [P, TJ, C])
        sc = s.sb("sc", [NE, T])

        dah = s.ps("dah", [P, 4, T])
        y = s.ps("y", [P, 2, T])
        wk = s.ps("wk", [P, 2, T])

        loads = [(w_in, w["in_T"]), (w_xd, w["xd_T"]), (w_xb, w["xb_T"]), (w_dt, w["dt_T"]),
                 (w_out, w["out_T"]), (w_g, w["g_T"]), (conv_w, w["conv_w"]), (conv_b, w["conv_b"]),
                 (dt_b, w["dt_b"]), (d_par, w["d_par"]), (a_log, w["a_log"]), (ident, w["ident"]),
                 (pick, w["pick"])]

        names = ("tick ld_w ld_x ld_xr st_x1 st_xn1 st_sc a_exp aneg const halo "
                 "bs agg ve rstd xn tr trev ix ixev cvc cv u iz izev sz xd xdev xb t1 xbev t2 t T dt dtev "
                 "ab ex sp de du bc bcev "
                 "dA dBu scan hC sum yt yg op x1 bs1 agg1 ve1 rstd1 xn1 pt ptev scm scev").split()
        S = {n: s.sem(n) for n in names}

        xv = x.rearrange("b (j p) c -> b p j c", p=P)
        x1v = x1.rearrange("(b j p) c -> b p j c", j=TJ, p=P)
        xn1v = xn1.rearrange("(b j p) c -> b p j c", j=TJ, p=P)
        scv = scores.rearrange("e (b t) -> b e t", t=T)

        run = ExitStack()
        block = run.enter_context(nc.Block())

        def batches(eng, prologue, body, epilogue):
            turns(eng, NB, prologue, lambda b, par, first, last: body(b, par, not first, not last), epilogue)

        @block.sync
        def _(sp_):
            for tile, src in loads:
                sp_.dma_start(tile[:], src).then_inc(S["ld_w"], 16)

            def load_x(b):
                sp_.dma_start(xt[:], xv[b]).then_inc(S["ld_x"], 16)

            def load_xr(b, first=False):
                if not first:
                    wait_alone(sp_, S["xn1"], b, S["tick"])
                    wait_alone(sp_, S["st_x1"], b * 16, S["tick"])
                sp_.dma_start(xr[:], xv[b]).then_inc(S["ld_xr"], 16)

            def store(b):
                wait_alone(sp_, S["x1"], b * 4 + 4, S["tick"])
                sp_.dma_start(x1v[b], x1t[:]).then_inc(S["st_x1"], 16)
                wait_alone(sp_, S["xn1"], b + 1, S["tick"])
                sp_.dma_start(xn1v[b], xn1t[:]).then_inc(S["st_xn1"], 16)
                wait_alone(sp_, S["scev"], b + 1, S["tick"])
                sp_.dma_start(scv[b], sc[:]).then_inc(S["st_sc"], 16)

            def prologue():
                load_x(0)
                load_xr(0, True)

            def body(b, par, post, prep):
                if prep:
                    wait_alone(sp_, S["xn"], b + 1, S["tick"])
                    load_x(b + 1)
                if post:
                    store(b - 1)
                    load_xr(b)

            def epilogue():
                store(NB - 1)
                sp_.wait_ge(S["st_x1"], NB * 16)
                sp_.wait_ge(S["st_xn1"], NB * 16)
                sp_.wait_ge(S["st_sc"], NB * 16)
                sp_.wait_ge(S["ld_x"], NB * 16)

            batches(sp_, prologue, body, epilogue)

        @block.scalar
        def _(act):
            def scan_exp(b, par, un):
                dt, n = un // NS, un % NS
                if n == 0:
                    act.wait_ge(S["de"], b * 4 + dt + 1)
                if not (isinstance(b, int) and b * UN + un < 4):
                    act.wait_ge(S["hC"], b * UN + un - 3)
                nc.scalar.activation(dah[:, un % 4, :], delta[:, par, dt, :], ACT.Exp,
                                     scale=a_neg[:, dt, n:n + 1]).then_inc(S["dA"], 1)

            def tr_out(b, k):
                act.wait_ge(S["tr"], b * 2 + k + 1)
                if not (isinstance(b, int) and b < 3):
                    act.wait_ge(S["scm"], b - 2)
                act.wait_ge(S["iz"], b * 4)
                nc.scalar.copy(xnT[:, k, :], wk[:, (k + 1) % 2, :]).then_inc(S["trev"], 1)

            def ix_out(b, dt):
                act.wait_ge(S["ix"], b * 4 + dt + 1)
                if dt >= 2 or not (isinstance(b, int) and b == 0):
                    act.wait_ge(S["cv"], b * 4 + dt - 1)
                nc.scalar.copy(xs[:, dt % 2, HALO:], wk[:, 1, :]).then_inc(S["ixev"], 1)

            def iz_out(b, par, dt):
                act.wait_ge(S["iz"], b * 4 + dt + 1)
                if not (isinstance(b, int) and b < 2):
                    act.wait_ge(S["yg"], b * 4 - 4)
                nc.scalar.copy(sz[:, par, dt, :], wk[:, 0, :]).then_inc(S["izev"], 1)

            def silus(b, par):
                act.wait_ge(S["cv"], b * 4 + 4)
                nc.scalar.activation(u[:, par, :, :], u[:, par, :, :], ACT.Silu).then_inc(S["u"], 1)
                act.wait_ge(S["izev"], b * 4 + 4)
                nc.scalar.activation(sz[:, par, :, :], sz[:, par, :, :], ACT.Silu).then_inc(S["sz"], 1)
                nc.scalar.preload_act_table_set("natural_log_exp_and_others")

            def xd_out(b):
                act.wait_ge(S["xd"], b + 1)
                act.wait_ge(S["dt"], b * 4)
                nc.scalar.copy(dtlo[:, :], wk[0:RK, 1, :]).then_inc(S["xdev"], 1)

            def softplus1(b, par, dt):
                act.wait_ge(S["dt"], b * 4 + dt + 1)
                if dt >= 2 or not (isinstance(b, int) and b == 0):
                    act.wait_ge(S["de"], b * 4 + dt - 1)
                v = wk[:, (dt + 1) % 2, :]
                nc.scalar.activation(sp[:, dt % 2, :], v, ACT.Abs, bias=dt_b[:, dt:dt + 1]).then_inc(S["ab"], 1)
                nc.scalar.activation(delta[:, par, dt, :], v, ACT.Relu,
                                     bias=dt_b[:, dt:dt + 1]).then_inc(S["dtev"], 1)

            def softplus2(b, dt):
                act.wait_ge(S["ab"], b * 4 + dt + 1)
                nc.scalar.activation(sp[:, dt % 2, :], sp[:, dt % 2, :], ACT.Exp, scale=-1.0).then_inc(S["ex"], 1)
                act.wait_ge(S["ex"], b * 4 + dt + 1)
                nc.scalar.activation(sp[:, dt % 2, :], sp[:, dt % 2, :], ACT.Ln, bias=1.0).then_inc(S["sp"], 1)

            def bc_out(b, j):
                act.wait_ge(S["bc"], b * 2 * NS + j + 1)
                if not (isinstance(b, int) and b == 0):
                    act.wait_ge(S["hC" if j % 2 else "dBu"], (b - 1) * UN + (KD - 1) * NS + j // 2 + 1)
                nc.scalar.copy(bc[:, j, :], wk[:, (j + 1) % 2, :]).then_inc(S["bcev"], 1)

            def pt_out(b, k):
                act.wait_ge(S["pt"], b * 2 + k + 1)
                if isinstance(b, int) and b >= NB - 2:
                    act.wait_ge(S["iz"], NB * 4)
                else:
                    act.wait_ge(S["iz"], (b + 3) * 4)
                if not (isinstance(b, int) and b == 0):
                    act.wait_ge(S["scm"], b)
                nc.scalar.copy(xnT[:, k, :], wk[:, k, :]).then_inc(S["ptev"], 1)

            def sc_out(b):
                act.wait_ge(S["scm"], b + 1)
                act.wait_ge(S["st_sc"], b * 16)
                nc.scalar.copy(sc[:, :], wk[0:NE, 0, :]).then_inc(S["scev"], 1)

            def prologue():
                nc.scalar.preload_act_table_set("natural_log_exp_and_others")
                act.wait_ge(S["ld_w"], 16 * len(loads))
                nc.scalar.activation(a_neg[:], a_log[:], ACT.Exp).then_inc(S["a_exp"], 1)
                act.wait_ge(S["a_exp"], 1)
                nc.scalar.mul(a_neg[:], a_neg[:], -1.0).then_inc(S["aneg"], 1)
                act.wait_ge(S["aneg"], 1)
                for k in range(KC):
                    tr_out(0, k)
                act.wait_ge(S["halo"], 1)
                for dt in range(KD):
                    ix_out(0, dt)
                    iz_out(0, 0, dt)
                silus(0, 0)
                xd_out(0)
                for dt in range(KD):
                    softplus1(0, 0, dt)
                    softplus2(0, dt)
                for j in range(2 * NS):
                    bc_out(0, j)

            def body(b, par, post, prep):
                for un in range(UN):
                    scan_exp(b, par, un)
                    if post and un < 4:
                        bc_out(b, 2 * (12 + un))
                        bc_out(b, 2 * (12 + un) + 1)
                    if prep:
                        if un in (14, 15):
                            tr_out(b + 1, un - 14)
                        if 16 <= un < 32 and un % 4 == 0:
                            ix_out(b + 1, (un - 16) // 4)
                        if 16 <= un < 32 and un % 4 == 2:
                            iz_out(b + 1, 1 - par, (un - 18) // 4)
                    if post and un in (32, 33):
                        pt_out(b - 1, un - 32)
                    if prep and un == 33:
                        silus(b + 1, 1 - par)
                    if post and un == 35:
                        sc_out(b - 1)
                    if prep:
                        if un == 39:
                            xd_out(b + 1)
                        if 43 <= un < 51:
                            if un % 2:
                                softplus1(b + 1, 1 - par, (un - 43) // 2)
                            else:
                                softplus2(b + 1, (un - 44) // 2)
                        if un >= 52:
                            bc_out(b + 1, 2 * (un - 52))
                            bc_out(b + 1, 2 * (un - 52) + 1)

            def epilogue():
                pt_out(NB - 1, 0)
                pt_out(NB - 1, 1)
                sc_out(NB - 1)

            batches(act, prologue, body, epilogue)

        @block.gpsimd
        def _(pool):
            def inv_std(b, var, ve_, rstd_, agg, sve, srs):
                wait_alone(pool, S[agg], b + 1, S["tick"])
                nc.gpsimd.tensor_scalar(ve_[:, :], var[:, :, 1], EPS, None, ALU.add).then_inc(S[sve], 1)
                wait_alone(pool, S[sve], b + 1, S["tick"])
                nc.gpsimd.tensor_tensor(rstd_[:, :], ve_[:, :], nhalf[:, :], ALU.pow).then_inc(S[srs], 1)

            def in_stats(b):
                inv_std(b, mv, ve, rstd, "agg", "ve", "rstd")

            def out_stats(b):
                inv_std(b, mv1, ve1, rstd1, "agg1", "ve1", "rstd1")

            def times_b(b, par, un):
                dt, n = un // NS, un % NS
                if n == 0:
                    pool.wait_ge(S["du"], b * 4 + dt + 1)
                if dt == 0:
                    pool.wait_ge(S["bcev"], b * 2 * NS + 2 * n + 1)
                if not (isinstance(b, int) and b * UN + un < 4):
                    pool.wait_ge(S["scan"], b * UN + un - 3)
                nc.gpsimd.tensor_tensor(dbu[:, un % 4, :], du[:, par, dt, :], bc[:, 2 * n, :],
                                        ALU.mult).then_inc(S["dBu"], 1)

            def prologue():
                nc.gpsimd.memset(nhalf[:], -0.5).then_inc(S["const"], 1)
                pool.wait_ge(S["const"], 1)
                in_stats(0)

            def body(b, par, post, prep):
                for un in range(UN):
                    times_b(b, par, un)
                    if post and un == 16:
                        out_stats(b - 1)
                    if prep and un == 5:
                        in_stats(b + 1)

            def epilogue():
                out_stats(NB - 1)

            batches(pool, prologue, body, epilogue)

        @block.vector
        def _(dve):
            def in_norm1(b):
                dve.wait_ge(S["ld_x"], b * 16 + 16)
                for j in range(TJ):
                    last = nc.vector.bn_stats(stat[:, j, :], xt[:, j, :])
                last.then_inc(S["bs"], 1)
                wait_alone(dve, S["bs"], b + 1, S["tick"])
                for j in range(TJ):
                    last = nc.vector.bn_aggr(mv[:, j, :], stat[:, j, :])
                last.then_inc(S["agg"], 1)

            def in_norm2(b):
                dve.wait_ge(S["rstd"], b + 1)
                dve.wait_ge(S["tr"], b * 2)
                for j in range(TJ):
                    last = nc.vector.tensor_scalar(xn[:, j, :], xt[:, j, :], mv[:, j, 0:1], rstd[:, j:j + 1],
                                                   ALU.subtract, ALU.mult)
                last.then_inc(S["xn"], 1)

            def conv(b, par, dt, k):
                o = u[:, par, dt, :]
                if k == 0:
                    dve.wait_ge(S["ixev"], b * 4 + dt + 1)
                    nc.vector.tensor_scalar(o, xs[:, dt % 2, 0:T], conv_w[:, dt, 0:1], conv_b[:, dt:dt + 1],
                                            ALU.mult, ALU.add).then_inc(S["cvc"], 1)
                else:
                    dve.wait_ge(S["cvc"], (b * 4 + dt) * HALO + k)
                    nc.vector.scalar_tensor_tensor(o, xs[:, dt % 2, k:k + T], conv_w[:, dt, k:k + 1], o,
                                                   ALU.mult, ALU.add).then_inc(S["cvc" if k < HALO else "cv"], 1)

            def split1(b):
                dve.wait_ge(S["xb"], b + 1)
                dve.wait_ge(S["bc"], b * 2 * NS)
                nc.vector.tensor_copy(bc1[:], wk[0:96, 0, :]).then_inc(S["t1"], 1)

            def split2(b):
                dve.wait_ge(S["t1"], b + 1)
                nc.vector.tensor_tensor(bcr[:], wk[0:96, 0, :], bc1[:], ALU.subtract).then_inc(S["xbev"], 1)

            def split3(b):
                dve.wait_ge(S["xbev"], b + 1)
                nc.vector.tensor_copy(bc2[:], bcr[:]).then_inc(S["t2"], 1)

            def split4(b):
                dve.wait_ge(S["t2"], b + 1)
                nc.vector.tensor_tensor(bc1[64:96, :], bcr[64:96, :], bc2[64:96, :], ALU.subtract)
                nc.vector.tensor_copy(bc1[32:64, :], bc2[32:64, :]).then_inc(S["T"], 1)

            splits = (split1, split2, split3, split4)

            def mk_delta(b, par, dt):
                dve.wait_ge(S["sp"], b * 4 + dt + 1)
                d = delta[:, par, dt, :]
                nc.vector.tensor_tensor(d, d, sp[:, dt % 2, :], ALU.add).then_inc(S["de"], 1)
                dve.wait_ge(S["de"], b * 4 + dt + 1)
                if dt == 0:
                    dve.wait_ge(S["u"], b + 1)
                    if not (isinstance(b, int) and b < 2):
                        dve.wait_ge(S["dBu"], b * UN - UN)
                nc.vector.tensor_tensor(du[:, par, dt, :], d, u[:, par, dt, :], ALU.mult).then_inc(S["du"], 1)

            def scan(b, par, un):
                g = b * UN + un
                dve.wait_ge(S["dA"], g + 1)
                dve.wait_ge(S["dBu"], g + 1)
                nc.vector.tensor_tensor_scan(dah[:, un % 4, :], dah[:, un % 4, :], dbu[:, un % 4, :], 0.0,
                                             ALU.mult, ALU.add).then_inc(S["scan"], 1)

            def times_c(b, par, un):
                dt, n = un // NS, un % NS
                g = b * UN + un
                dve.wait_ge(S["scan"], g + 1)
                if dt == 0:
                    dve.wait_ge(S["bcev"], b * 2 * NS + 2 * n + 2)
                if not (isinstance(b, int) and b * UN + un < 4):
                    dve.wait_ge(S["sum"], g - 3)
                nc.vector.tensor_tensor(hc[:, un % 4, :], dah[:, un % 4, :], bc[:, 2 * n + 1, :],
                                        ALU.mult).then_inc(S["hC"], 1)

            def gate(b, par, dt):
                dve.wait_ge(S["sum"], b * UN + (dt + 1) * NS)
                if dt == 0:
                    dve.wait_ge(S["u"], b + 1)
                    dve.wait_ge(S["sz"], b + 1)
                    dve.wait_ge(S["op"], b * 4)
                nc.vector.scalar_tensor_tensor(yg[:, dt, :], u[:, par, dt, :], d_par[:, dt:dt + 1], y[:, dt % 2, :],
                                               ALU.mult, ALU.add).then_inc(S["yt"], 1)
                dve.wait_ge(S["yt"], b * 4 + dt + 1)
                nc.vector.tensor_tensor(yg[:, dt, :], yg[:, dt, :], sz[:, par, dt, :], ALU.mult).then_inc(S["yg"], 1)

            def residual(b, j):
                dve.wait_ge(S["op"], b * 4 + j + 1)
                if j == 0:
                    dve.wait_ge(S["ld_xr"], b * 16 + 16)
                nc.vector.tensor_tensor(x1t[:, j, :], wk[:, j % 2, 0:C], xr[:, j, :], ALU.add).then_inc(S["x1"], 1)

            def out_norm1(b):
                dve.wait_ge(S["x1"], b * 4 + 4)
                for j in range(TJ):
                    last = nc.vector.bn_stats(stat1[:, j, :], x1t[:, j, :])
                last.then_inc(S["bs1"], 1)
                wait_alone(dve, S["bs1"], b + 1, S["tick"])
                for j in range(TJ):
                    last = nc.vector.bn_aggr(mv1[:, j, :], stat1[:, j, :])
                last.then_inc(S["agg1"], 1)

            def out_norm2(b):
                dve.wait_ge(S["rstd1"], b + 1)
                dve.wait_ge(S["pt"], b * 2)
                dve.wait_ge(S["st_xn1"], b * 16)
                for j in range(TJ):
                    last = nc.vector.tensor_scalar(xn1t[:, j, :], x1t[:, j, :], mv1[:, j, 0:1], rstd1[:, j:j + 1],
                                                   ALU.subtract, ALU.mult)
                last.then_inc(S["xn1"], 1)

            def prologue():
                nc.vector.memset(xs[:, :, 0:HALO], 0.0).then_inc(S["halo"], 1)
                dve.wait_ge(S["halo"], 1)
                dve.wait_ge(S["ld_w"], 16 * len(loads))
                nc.vector.tensor_copy(pickb[:], pick[:]).then_inc(S["halo"], 1)
                in_norm1(0)
                in_norm2(0)
                for dt in range(KD):
                    for k in range(CW):
                        conv(0, 0, dt, k)
                for split in splits:
                    split(0)
                for dt in range(KD):
                    mk_delta(0, 0, dt)

            def body(b, par, post, prep):
                for un in range(UN):
                    scan(b, par, un)
                    if un:
                        times_c(b, par, un - 1)
                    if un in (18, 34, 50):
                        gate(b, par, (un - 18) // 16)
                    if post:
                        if un == 1:
                            gate(b - 1, 1 - par, KD - 1)
                        if un in (3, 5, 7, 9):
                            residual(b - 1, (un - 3) // 2)
                        if un == 11:
                            out_norm1(b - 1)
                        if un == 18:
                            out_norm2(b - 1)
                    if prep:
                        if un == 0:
                            in_norm1(b + 1)
                        if un == 7:
                            in_norm2(b + 1)
                        if 14 <= un < 30:
                            conv(b + 1, 1 - par, (un - 14) // CW, (un - 14) % CW)
                        if 37 <= un < 41:
                            splits[un - 37](b + 1)
                        if un in (43, 45, 47, 49):
                            mk_delta(b + 1, 1 - par, (un - 43) // 2)
                times_c(b, par, UN - 1)

            def epilogue():
                gate(NB - 1, (NB - 1) % 2, KD - 1)
                for j in range(TJ):
                    residual(NB - 1, j)
                out_norm1(NB - 1)
                out_norm2(NB - 1)

            batches(dve, prologue, body, epilogue)

        @block.tensor
        def _(pe):
            def mm(out, lhsT, rhs, first, last):
                return nc.tensor.matmul(out, lhsT, rhs, start=first, stop=last)

            def tr(b, k):
                pe.wait_ge(S["xn"], b + 1)
                for j in range(TJ):
                    last = nc.tensor.transpose(wk[:, (k + 1) % 2, j * P:(j + 1) * P],
                                               xn[:, j, k * P:(k + 1) * P], ident[:])
                last.then_inc(S["tr"], 1)

            def ix(b, dt):
                if dt == 0:
                    pe.wait_ge(S["trev"], b * 2 + 2)
                else:
                    pe.wait_ge(S["ixev"], b * 4 + dt)
                for k in range(KC):
                    last = mm(wk[:, 1, :], w_in[:, k, dt * P:(dt + 1) * P], xnT[:, k, :], k == 0, k == KC - 1)
                last.then_inc(S["ix"], 1)

            def iz(b, dt):
                if dt:
                    pe.wait_ge(S["izev"], b * 4 + dt)
                for k in range(KC):
                    last = mm(wk[:, 0, :], w_in[:, k, DI + dt * P:DI + (dt + 1) * P], xnT[:, k, :],
                              k == 0, k == KC - 1)
                last.then_inc(S["iz"], 1)

            def xd(b, par):
                pe.wait_ge(S["u"], b + 1)
                for k in range(KD):
                    last = mm(wk[0:RK, 1, :], w_xd[:, k, :], u[:, par, k, :], k == 0, k == KD - 1)
                last.then_inc(S["xd"], 1)

            def xb(b, par, post):
                if post:
                    pe.wait_ge(S["scev"], b - 1)
                else:
                    pe.wait_ge(S["izev"], b * 4 + 4)
                for k in range(KD):
                    last = mm(wk[0:96, 0, :], w_xb[:, k, :], u[:, par, k, :], k == 0, k == KD - 1)
                last.then_inc(S["xb"], 1)

            def dtp(b, dt):
                if dt == 0:
                    pe.wait_ge(S["xdev"], b + 1)
                elif dt == 1:
                    pe.wait_ge(S["xbev"], b + 1)
                else:
                    pe.wait_ge(S["dtev"], b * 4 + dt - 1)
                mm(wk[:, (dt + 1) % 2, :], w_dt[:, dt * P:(dt + 1) * P], dtlo[:, :], True, True)\
                    .then_inc(S["dt"], 1)

            def bcast(b, j):
                if j == 0:
                    pe.wait_ge(S["T"], b + 1)
                if j < 2:
                    pe.wait_ge(S["dtev"], b * 4 + j + 3)
                else:
                    pe.wait_ge(S["bcev"], b * 2 * NS + j - 1)
                row = j // 2 + (NS if j % 2 else 0)
                mm(wk[:, (j + 1) % 2, :], pickb[:, row:row + 1].to_broadcast([96, P]), bc1[:], True, True)\
                    .then_inc(S["bc"], 1)

            def total(b, un):
                dt, n = un // NS, un % NS
                g = b * UN + un
                if n == 0 and not (isinstance(b, int) and b == 0 and dt < 2):
                    pe.wait_ge(S["yg"], b * 4 + dt - 1)
                pe.wait_ge(S["hC"], g + 1)
                mm(y[:, dt % 2, :], ident[:], hc[:, un % 4, :], n == 0, n == NS - 1).then_inc(S["sum"], 1)

            def outp(b, j, ending=False):
                if j == 0:
                    pe.wait_ge(S["yg"], b * 4 + 4)
                if j < 2:
                    if ending:
                        pe.wait_ge(S["scev"], NB - 1)
                        pe.wait_ge(S["ptev"], 2 * (NB - 1))
                    else:
                        pe.wait_ge(S["bcev"], (b + 2) * 2 * NS)
                else:
                    pe.wait_ge(S["x1"], b * 4 + j - 1)
                for k in range(KD):
                    last = mm(wk[:, j % 2, 0:C], yg[:, k, j * P:(j + 1) * P], w_out[:, k, :], k == 0, k == KD - 1)
                last.then_inc(S["op"], 1)

            def ptr(b, k, prep):
                pe.wait_ge(S["xn1"], b + 1)
                if prep:
                    pe.wait_ge(S["ixev" if k else "izev"], (b + 3) * 4)
                for j in range(TJ):
                    last = nc.tensor.transpose(wk[:, k, j * P:(j + 1) * P], xn1t[:, j, k * P:(k + 1) * P], ident[:])
                last.then_inc(S["pt"], 1)

            def gate_scores(b):
                pe.wait_ge(S["ptev"], b * 2 + 2)
                for k in range(KC):
                    last = mm(wk[0:NE, 0, :], w_g[:, k, :], xnT[:, k, :], k == 0, k == KC - 1)
                last.then_inc(S["scm"], 1)

            def prologue():
                pe.wait_ge(S["ld_w"], 16 * len(loads))
                for k in range(KC):
                    tr(0, k)
                for dt in range(KD):
                    ix(0, dt)
                    iz(0, dt)
                xd(0, 0)
                xb(0, 0, False)
                for dt in range(KD):
                    dtp(0, dt)
                for j in range(2 * NS):
                    bcast(0, j)

            def body(b, par, post, prep):
                for un in range(UN):
                    if un:
                        total(b, un - 1)
                    if post:
                        if un == 0:
                            bcast(b, 30)
                            bcast(b, 31)
                        if un in (2, 4, 6, 8):
                            outp(b - 1, (un - 2) // 2)
                    if prep:
                        if un == 10:
                            if post:
                                pe.wait_ge(S["x1"], b * 4)
                            else:
                                pe.wait_ge(S["bcev"], 2 * NS)
                        if un in (10, 11):
                            tr(b + 1, un - 10)
                        if 12 <= un < 28 and un % 4 == 0:
                            ix(b + 1, (un - 12) // 4)
                        if 12 <= un < 28 and un % 4 == 2:
                            iz(b + 1, (un - 14) // 4)
                    if post:
                        if un in (28, 29):
                            ptr(b - 1, un - 28, prep)
                        if un == 31:
                            gate_scores(b - 1)
                    if prep:
                        if un == 35:
                            xd(b + 1, 1 - par)
                        if un == 36:
                            xb(b + 1, 1 - par, post)
                        if un in (39, 41, 43, 45):
                            dtp(b + 1, (un - 39) // 2)
                        if un >= 49:
                            bcast(b + 1, 2 * (un - 49))
                            bcast(b + 1, 2 * (un - 49) + 1)
                total(b, UN - 1)

            def epilogue():
                for j in range(TJ):
                    outp(NB - 1, j, True)
                for k in range(KC):
                    ptr(NB - 1, k, False)
                gate_scores(NB - 1)

            batches(pe, prologue, body, epilogue)
        run.close()
        s.clear()


def below(i, n):
    return isinstance(i, int) and i < n


def wait_alone(eng, sem, value, tick):
    eng.wait_ge(sem, value)
    eng.sem_inc(tick, 1)


def choose(nc, name, scores, w, slot_tok, slot_w):
    NBITS = 31
    with ExitStack() as keep:
        k = Scope(nc, keep, name)
        lo = k.sb("lo", [P, T], BF16)
        hi = k.sb("hi", [P, T], BF16)
        wp = k.sb("wp", [P, 3, T], BF16)
        with ExitStack() as stack:
            s = Scope(nc, stack, name + "a")
            sc = s.sb("sc", [P, T])
            blk = s.sb("blk", [P, P])
            low = s.sb("low", [P, P])
            ident = s.sb("ident", [P, P])
            bitf = s.sb("bitf", [P, NBITS + 1])
            biti = s.sb("biti", [P, NBITS + 1], I32)
            one = s.sb("one", [P, T])
            junk = s.sb("junk", [P, T])
            rmax = s.sb("rmax", [P, 1])
            emax = s.sb("emax", [1, NE])
            emax_b = s.sb("emax_b", [1, NE, NB])
            nmax = s.sb("nmax", [P, 1])
            cnt = s.sb("cnt", [P, 1])
            hit = s.sb("hit", [P, 1], I32)
            found = s.sb("found", [P, 1], I32)
            trial = s.sb("trial", [P, 1], I32)
            gt = s.sb("gt", [P, T])
            eq = s.sb("eq", [P, T])
            cg = s.sb("cg", [P, 1])
            ce = s.sb("ce", [P, 1])
            need = s.sb("need", [P, 1])
            offe = s.sb("offe", [P, 1])
            pe_ = s.sb("pe", [P, T])
            sele = s.sb("sele", [P, T])
            sel = s.sb("sel", [P, T])
            rows = s.sb("rows", [P, 1])
            offs = s.sb("offs", [P, 1])
            ps_ = s.sb("ps", [P, T])
            pos = s.sb("pos", [P, T])
            ex = s.sb("ex", [P, T])
            ew = s.sb("ew", [P, T])
            sw = s.sb("sw", [P, 1])
            rw = s.sb("rw", [P, 1])
            wgt = s.sb("wgt", [P, T])
            posi = s.sb("posi", [P, T], I32)
            loi = s.sb("loi", [P, T], I32)
            hii = s.sb("hii", [P, T], I32)
            wr = s.sb("wr", [P, T])
            tot = s.ps("tot", [P, 512])
            mrow = s.ps("mrow", [P, 512])
            mcol = s.ps("mcol", [P, 512])
            offp = s.ps("offp", [P, 512])
            tpos = s.ps("tpos", [P, T])
            twgt = s.ps("twgt", [P, T])
            S = {n: s.sem(n) for n in
                 "ld one rmax mrow emax emb mcol nmax cnt tot hit trial found masks offp small pe sele sel offs "
                 "ps pos ex ew sw rw wgt tp tw posi loi hii w1 wr w2 wr2 done".split()}
            consts = [(blk, w["blk"]), (low, w["low"]), (ident, w["ident"]), (bitf, w["bitf"]), (biti, w["biti"])]
            run = ExitStack()
            block = run.enter_context(nc.Block())

            @block.sync
            def _(sp):
                sp.dma_start(sc[:], scores.rearrange("e (b t) -> (e b) t", t=T)).then_inc(S["ld"], 16)
                for tile, src in consts:
                    sp.dma_start(tile[:], src).then_inc(S["ld"], 16)

            loaded = 16 * (1 + len(consts))

            @block.scalar
            def _(act):
                act.wait_ge(S["nmax"], 1)
                nc.scalar.activation(ex[:], sc[:], ACT.Exp, bias=nmax[:, 0:1]).then_inc(S["ex"], 1)

            @block.tensor
            def _(pe):
                pe.wait_ge(S["rmax"], 1)
                nc.tensor.transpose(mrow[0:1, 0:P], rmax[:], ident[:]).then_inc(S["mrow"], 1)
                pe.wait_ge(S["emb"], 1)
                nc.tensor.matmul(mcol[:, 0:1], emax_b[:, :, :].rearrange("p e b -> p (e b)"), one[0:1, 0:1],
                                 start=True, stop=True).then_inc(S["mcol"], 1)

                def total_of(r):
                    pe.wait_ge(S["cnt"], r + 1)
                    nc.tensor.matmul(tot[:, 0:1], blk[:], cnt[:], start=True, stop=True).then_inc(S["tot"], 1)

                total_of(0)
                with pe.Fori(0, NBITS) as i:
                    total_of(i + 1)
                pe.wait_ge(S["masks"], 2)
                nc.tensor.matmul(tot[:, 0:1], blk[:], cg[:], start=True, stop=True).then_inc(S["tot"], 1)
                nc.tensor.matmul(offp[:, 0:1], low[:], ce[:], start=True, stop=True).then_inc(S["offp"], 1)
                pe.wait_ge(S["sel"], 1)
                nc.tensor.matmul(mcol[:, 0:1], low[:], rows[:], start=True, stop=True).then_inc(S["offs"], 1)
                pe.wait_ge(S["ew"], 1)
                nc.tensor.matmul(mrow[:, 0:1], blk[:], sw[:], start=True, stop=True).then_inc(S["sw"], 1)
                pe.wait_ge(S["pos"], 1)
                for j in range(TJ):
                    last = nc.tensor.transpose(tpos[:, j * P:(j + 1) * P], pos[:, j * P:(j + 1) * P], ident[:])
                last.then_inc(S["tp"], 1)
                pe.wait_ge(S["wgt"], 1)
                for j in range(TJ):
                    last = nc.tensor.transpose(twgt[:, j * P:(j + 1) * P], wgt[:, j * P:(j + 1) * P], ident[:])
                last.then_inc(S["tw"], 1)

            @block.vector
            def _(dve):
                V = nc.vector
                V.memset(one[:], 1.0).then_inc(S["one"], 1)
                dve.wait_ge(S["one"], 1)
                dve.wait_ge(S["ld"], loaded)
                V.tensor_reduce(rmax[:], sc[:], AX.X, ALU.max).then_inc(S["rmax"], 1)
                dve.wait_ge(S["mrow"], 1)
                V.tensor_reduce(emax[:], mrow[0:1, 0:P].rearrange("p (e b) -> p e b", b=NB), AX.X, ALU.max)\
                    .then_inc(S["emax"], 1)
                dve.wait_ge(S["emax"], 1)
                V.tensor_copy(emax_b[:], emax[:].rearrange("p (e o) -> p e o", o=1).to_broadcast([1, NE, NB]))\
                    .then_inc(S["emb"], 1)
                dve.wait_ge(S["mcol"], 1)
                V.tensor_scalar(nmax[:], mcol[:, 0:1], -1.0, None, ALU.mult).then_inc(S["nmax"], 1)

                V.tensor_scalar(junk[:], sc[:], 0.0, None, ALU.is_ge, ALU.add, accum_out=cnt[:])\
                    .then_inc(S["cnt"], 1)
                dve.wait_ge(S["tot"], 1)
                V.tensor_scalar(found[:], tot[:, 0:1], float(CAP), -1.0, ALU.is_ge, ALU.add)\
                    .then_inc(S["found"], 1)
                dve.wait_ge(S["found"], 1)
                V.tensor_tensor(trial[:], found[:], biti[:, 0:1], ALU.bitwise_xor).then_inc(S["trial"], 1)
                with dve.Fori(0, NBITS) as i:
                    dve.wait_ge(S["trial"], i + 1)
                    V.tensor_scalar(junk[:], sc[:], trial[:].bitcast(F32), None, ALU.is_ge, ALU.add,
                                    accum_out=cnt[:]).then_inc(S["cnt"], 1)
                    dve.wait_ge(S["tot"], i + 2)
                    V.tensor_scalar(hit[:], tot[:, 0:1], float(CAP), bitf[:, bass.ds(i, 1)], ALU.is_ge, ALU.mult)\
                        .then_inc(S["hit"], 1)
                    dve.wait_ge(S["hit"], i + 1)
                    V.scalar_tensor_tensor(trial[:], hit[:], biti[:, bass.ds(i + 1, 1)], found[:],
                                           ALU.bitwise_xor, ALU.bitwise_xor).then_inc(S["trial"], 1)
                    V.tensor_tensor(found[:], hit[:], found[:], ALU.bitwise_xor).then_inc(S["found"], 1)
                dve.wait_ge(S["trial"], NBITS + 1)
                dve.wait_ge(S["found"], NBITS + 1)
                thr = found[:].bitcast(F32)
                V.tensor_scalar(gt[:], sc[:], thr, None, ALU.is_gt, ALU.add, accum_out=cg[:]).then_inc(S["masks"], 1)
                V.tensor_scalar(eq[:], sc[:], thr, None, ALU.is_equal, ALU.add, accum_out=ce[:]).then_inc(S["masks"], 1)
                dve.wait_ge(S["tot"], NBITS + 2)
                V.tensor_scalar(need[:], tot[:, 0:1], -1.0, float(CAP), ALU.mult, ALU.add).then_inc(S["small"], 1)
                dve.wait_ge(S["offp"], 1)
                V.tensor_copy(offe[:], offp[:, 0:1]).then_inc(S["small"], 1)
                dve.wait_ge(S["small"], 2)
                dve.wait_ge(S["masks"], 2)
                V.tensor_tensor_scan(pe_[:], one[:], eq[:], offe[:, 0:1], ALU.mult, ALU.add).then_inc(S["pe"], 1)
                dve.wait_ge(S["pe"], 1)
                V.scalar_tensor_tensor(sele[:], pe_[:], need[:, 0:1], eq[:], ALU.is_le, ALU.mult)\
                    .then_inc(S["sele"], 1)
                dve.wait_ge(S["sele"], 1)
                V.scalar_tensor_tensor(sel[:], sele[:], 1.0, gt[:], ALU.mult, ALU.add, accum_out=rows[:])\
                    .then_inc(S["sel"], 1)
                dve.wait_ge(S["sel"], 1)
                dve.wait_ge(S["ex"], 1)
                V.scalar_tensor_tensor(ew[:], ex[:], 1.0, sel[:], ALU.mult, ALU.mult, accum_out=sw[:])\
                    .then_inc(S["ew"], 1)
                dve.wait_ge(S["offs"], 1)
                V.tensor_copy(offs[:], mcol[:, 0:1]).then_inc(S["small"], 1)
                dve.wait_ge(S["small"], 3)
                V.tensor_tensor_scan(ps_[:], one[:], sel[:], offs[:, 0:1], ALU.mult, ALU.add).then_inc(S["ps"], 1)
                dve.wait_ge(S["ps"], 1)
                V.tensor_tensor(pos[:], ps_[:], sel[:], ALU.mult).then_inc(S["pos"], 1)
                dve.wait_ge(S["sw"], 1)
                V.reciprocal(rw[:], mrow[:, 0:1]).then_inc(S["rw"], 1)
                dve.wait_ge(S["rw"], 1)
                dve.wait_ge(S["ew"], 1)
                V.tensor_scalar(wgt[:], ew[:], rw[:, 0:1], None, ALU.mult).then_inc(S["wgt"], 1)
                dve.wait_ge(S["tp"], 1)
                V.tensor_scalar(posi[:], tpos[:], -1.0, None, ALU.add).then_inc(S["posi"], 1)
                dve.wait_ge(S["posi"], 1)
                V.tensor_scalar(loi[:], posi[:], 7, None, ALU.arith_shift_right).then_inc(S["loi"], 1)
                V.tensor_scalar(hii[:], posi[:], P - 1, None, ALU.bitwise_and).then_inc(S["hii"], 1)
                dve.wait_ge(S["loi"], 1)
                V.tensor_copy(lo[:], loi[:]).then_inc(S["done"], 1)
                dve.wait_ge(S["hii"], 1)
                V.tensor_copy(hi[:], hii[:]).then_inc(S["done"], 1)
                dve.wait_ge(S["tw"], 1)
                V.tensor_copy(wp[:, 0, :], twgt[:]).then_inc(S["w1"], 1)
                dve.wait_ge(S["w1"], 1)
                V.tensor_tensor(wr[:], twgt[:], wp[:, 0, :], ALU.subtract).then_inc(S["wr"], 1)
                dve.wait_ge(S["wr"], 1)
                V.tensor_copy(wp[:, 1, :], wr[:]).then_inc(S["w2"], 1)
                dve.wait_ge(S["w2"], 1)
                V.tensor_tensor(wp[:, 2, :], wr[:], wp[:, 1, :], ALU.subtract).then_inc(S["done"], 1)
            run.close()
            s.clear()

        with ExitStack() as stack:
            s = Scope(nc, stack, name + "b")
            NV = 5
            hot = s.sb("hot", [P, P, T], BF16)
            lhot = s.sb("lhot", [P, NSLOT, T], BF16)
            val = s.sb("val", [P, NV, NSLOT, T], BF16)
            part = s.sb("part", [P, 1])
            tilei = s.sb("tilei", [P, TJ, NE, NB], I32)
            tileb = s.sb("tileb", [P, T], BF16)
            col = s.sb("col", [P, P])
            got = s.sb("got", [P, NE, NV, NSLOT])
            tokf = s.sb("tokf", [P, NE, NSLOT])
            w12 = s.sb("w12", [P, NE, NSLOT])
            acc = s.ps("acc", [P, NE, NV, NSLOT])
            S = {n: s.sem(n) for n in "ld iota tile lhot val hot acc got tok w12 out".split()}
            run = ExitStack()
            block = run.enter_context(nc.Block())

            @block.sync
            def _(sp):
                sp.dma_start(part[:], w["part"]).then_inc(S["ld"], 16)
                sp.dma_start(col[:], w["col"]).then_inc(S["ld"], 16)

            @block.gpsimd
            def _(pool):
                nc.gpsimd.iota(tilei[:], pattern=[[1, TJ], [0, NE], [TJ, NB]], base=0, channel_multiplier=0)\
                    .then_inc(S["iota"], 1)
                pool.wait_ge(S["iota"], 1)
                nc.gpsimd.tensor_copy(tileb[:], tilei[:].rearrange("p j e b -> p (j e b)")).then_inc(S["tile"], 1)

            @block.vector
            def _(dve):
                V = nc.vector
                dve.wait_ge(S["ld"], 32)
                for l in range(NSLOT):
                    V.tensor_scalar(lhot[:, l, :], lo[:], float(l), None, ALU.is_equal).then_inc(S["lhot"], 1)
                with dve.Fori(0, P // 8) as i:
                    for q in range(8):
                        V.tensor_scalar(hot[:, bass.ds(i * 8 + q, 1), :].rearrange("p o t -> p (o t)"), hi[:],
                                        col[:, bass.ds(i * 8 + q, 1)], None, ALU.is_equal).then_inc(S["hot"], 1)
                dve.wait_ge(S["lhot"], NSLOT)
                V.tensor_scalar(val[:, 0, :, :], lhot[:], part[:, 0:1], None, ALU.mult).then_inc(S["val"], 1)
                dve.wait_ge(S["tile"], 1)
                for v, src in ((1, tileb[:]), (2, wp[:, 0, :]), (3, wp[:, 1, :]), (4, wp[:, 2, :])):
                    V.tensor_tensor(val[:, v, :, :], lhot[:],
                                    src.rearrange("p (o t) -> p o t", o=1).to_broadcast([P, NSLOT, T]),
                                    ALU.mult).then_inc(S["val"], 1)
                dve.wait_ge(S["acc"], NE)
                V.tensor_copy(got[:], acc[:]).then_inc(S["got"], 1)
                dve.wait_ge(S["got"], 1)
                V.tensor_scalar(tokf[:], got[:, :, 1, :], float(P), None, ALU.mult).then_inc(S["tok"], 1)
                V.tensor_tensor(w12[:], got[:, :, 2, :], got[:, :, 3, :], ALU.add).then_inc(S["w12"], 1)
                dve.wait_ge(S["tok"], 1)
                V.tensor_tensor(slot_tok[:].rearrange("p (e l) -> p e l", l=NSLOT), tokf[:], got[:, :, 0, :],
                                ALU.add).then_inc(S["out"], 1)
                dve.wait_ge(S["w12"], 1)
                V.tensor_tensor(slot_w[:].rearrange("p (e l) -> p e l", l=NSLOT), w12[:], got[:, :, 4, :],
                                ALU.add).then_inc(S["out"], 1)

            @block.tensor
            def _(pe):
                pe.wait_ge(S["hot"], P)
                pe.wait_ge(S["val"], NV)
                for e in range(NE):
                    for n in range(NB * TJ):
                        c = (n % TJ) * P + e * NB + n // TJ
                        last = nc.tensor.matmul(acc[:, e, :, :], hot[:, :, c], val[:, :, :, c],
                                                start=n == 0, stop=n == NB * TJ - 1)
                    last.then_inc(S["acc"], 1)
            run.close()
            s.clear()


def experts(nc, name, xn, res, w, slot_tok, slot_w):
    with ExitStack() as stack:
        s = Scope(nc, stack, name)
        w1 = s.sb("w1", [P, 2, KC, FH])
        w3 = s.sb("w3", [P, 2, KC, FH])
        w2 = s.sb("w2", [P, 2, KF, C])
        ident = s.sb("ident", [P, P])
        tok = s.sb("tok", [P, 2, NSLOT], I32)
        xg = s.sb("xg", [P, 2, NSLOT, C])
        xgT = s.sb("xgT", [P, 2, KC, CAP])
        sg = s.sb("sg", [P, 2, T])
        hT = s.sb("hT", [P, 2, KF, T])
        yo = s.sb("yo", [P, 2, NSLOT, C])
        tp = s.ps("tp", [P, 2, T])
        h1 = s.ps("h1", [P, 2, T])
        h3 = s.ps("h3", [P, 2, T])
        yp = s.ps("yp", [P, 2, T])
        S = {n: s.sem(n) for n in "tick ld_id ld0 ld1 tok g0 g1 tr xev h sg mul y ye sc".split()}
        run = ExitStack()
        block = run.enter_context(nc.Block())
        HALVES = CAP // T
        NH_ = HALVES * KF

        @block.sync
        def _(sp):
            def body(e, q, first, last):
                if not below(e, 2):
                    sp.wait_ge(S["y"], (e - 1) * NSLOT)
                sp.dma_start(w1[:, q, :, :], w["w1"][e]).then_inc(S[f"ld{q}"], 16)
                sp.dma_start(w3[:, q, :, :], w["w3"][e]).then_inc(S[f"ld{q}"], 16)
                sp.dma_start(w2[:, q, :, :], w["w2"][e]).then_inc(S[f"ld{q}"], 16)

            def prologue():
                sp.dma_start(ident[:], w["ident"]).then_inc(S["ld_id"], 16)

            turns(sp, NE, prologue, body, lambda: None)

        def loads_by(e, q):
            return 48 * (e // 2 + 1) if isinstance(e, int) else (e - q) * 24 + 48

        def gathers_by(e, q):
            return 16 * NSLOT * (e // 2 + 1) if isinstance(e, int) else (e - q) * (8 * NSLOT) + 16 * NSLOT

        @block.gpsimd
        def _(pool):
            def gather(e, q):
                if not below(e, 2):
                    pool.wait_ge(S["tr"], (e - 1) * 4)
                    pool.wait_ge(S["sc"], (e - 1) * 16 * NSLOT)
                nc.gpsimd.tensor_copy(tok[:, q, :], slot_tok[:, bass.ds(e * NSLOT, NSLOT)]).then_inc(S["tok"], 1)
                wait_alone(pool, S["tok"], e + 1, S["tick"])
                for l in range(NSLOT):
                    nc.gpsimd.indirect_dma_start(
                        xg[:, q, l, :], None, xn, bass.IndirectOffsetOnAxis(tok[:, q, l:l + 1], 0),
                    ).then_inc(S[f"g{q}"], 16)

            def scatter(e, q):
                if not below(e, 1):
                    pool.wait_ge(S["sc"], e * 16 * NSLOT)
                for l in range(NSLOT):
                    wait_alone(pool, S["ye"], e * NSLOT + l + 1, S["tick"])
                    nc.gpsimd.indirect_dma_start(
                        res, bass.IndirectOffsetOnAxis(tok[:, q, l:l + 1], 0), yo[:, q, l, :], None,
                        compute_op=ALU.add).then_inc(S["sc"], 16)

            def body(e, q, first, last):
                gather(e, q)
                if not first:
                    scatter(e - 1, 1 - q)

            def epilogue():
                scatter(NE - 1, (NE - 1) % 2)
                pool.wait_ge(S["sc"], NE * 16 * NSLOT)

            turns(pool, NE, lambda: None, body, epilogue)

        @block.tensor
        def _(pe):
            def transposes(e, q):
                pe.wait_ge(S[f"g{q}"], gathers_by(e, q))
                for g in range(4):
                    k, half = g % 2, g // 2
                    if not below(e * 4 + g, 2):
                        pe.wait_ge(S["xev"], e * 4 + g - 1)
                    for j in range(TJ):
                        last = nc.tensor.transpose(tp[:, g % 2, j * P:(j + 1) * P],
                                                   xg[:, q, half * TJ + j, k * P:(k + 1) * P], ident[:])
                    last.then_inc(S["tr"], 1)

            def hidden(e, q):
                pe.wait_ge(S[f"ld{q}"], loads_by(e, q))
                pe.wait_ge(S["xev"], e * 4 + 4)
                for m in range(NH_):
                    half, f = m // KF, m % KF
                    if not below(e * NH_ + m, 2):
                        pe.wait_ge(S["mul"], e * NH_ + m - 1)
                    for wt, out in ((w1, h1), (w3, h3)):
                        for k in range(KC):
                            last = nc.tensor.matmul(out[:, m % 2, :], wt[:, q, k, f * P:(f + 1) * P],
                                                    xgT[:, q, k, half * T:(half + 1) * T],
                                                    start=k == 0, stop=k == KC - 1)
                    last.then_inc(S["h"], 1)

            def outputs(e, q):
                for l in range(NSLOT):
                    half, j = l // TJ, l % TJ
                    if j == 0:
                        pe.wait_ge(S["mul"], e * NH_ + (half + 1) * KF)
                    if not below(e * NSLOT + l, 2):
                        pe.wait_ge(S["ye"], e * NSLOT + l - 1)
                    for f in range(KF):
                        last = nc.tensor.matmul(yp[:, l % 2, 0:C], hT[:, half, f, j * P:(j + 1) * P],
                                                w2[:, q, f, :], start=f == 0, stop=f == KF - 1)
                    last.then_inc(S["y"], 1)

            def prologue():
                pe.wait_ge(S["ld_id"], 16)
                transposes(0, 0)

            def body(e, q, first, last):
                hidden(e, q)
                if not last:
                    transposes(e + 1, 1 - q)
                outputs(e, q)

            turns(pe, NE, prologue, body, lambda: None)

        @block.scalar
        def _(act):
            def tokens_out(e, q):
                for g in range(4):
                    k, half = g % 2, g // 2
                    act.wait_ge(S["tr"], e * 4 + g + 1)
                    if g == 0 and not below(e, 2):
                        act.wait_ge(S["h"], (e - 1) * NH_)
                    nc.scalar.copy(xgT[:, q, k, half * T:(half + 1) * T], tp[:, g % 2, :]).then_inc(S["xev"], 1)

            def silus(e, q):
                for m in range(NH_):
                    act.wait_ge(S["h"], e * NH_ + m + 1)
                    if not below(e * NH_ + m, 2):
                        act.wait_ge(S["mul"], e * NH_ + m - 1)
                    nc.scalar.activation(sg[:, m % 2, :], h1[:, m % 2, :], ACT.Silu).then_inc(S["sg"], 1)

            def body(e, q, first, last):
                silus(e, q)
                if not last:
                    tokens_out(e + 1, 1 - q)

            turns(act, NE, lambda: tokens_out(0, 0), body, lambda: None)

        @block.vector
        def _(dve):
            def body(e, q, first, last):
                for m in range(NH_):
                    half, f = m // KF, m % KF
                    dve.wait_ge(S["sg"], e * NH_ + m + 1)
                    if f == 0 and not first:
                        dve.wait_ge(S["y"], e * NSLOT + half * TJ + TJ - NSLOT)
                    nc.vector.tensor_tensor(hT[:, half, f, :], sg[:, m % 2, :], h3[:, m % 2, :], ALU.mult)\
                        .then_inc(S["mul"], 1)
                for l in range(NSLOT):
                    dve.wait_ge(S["y"], e * NSLOT + l + 1)
                    if l == 0 and not below(e, 2):
                        dve.wait_ge(S["sc"], (e - 1) * 16 * NSLOT)
                    nc.vector.tensor_scalar(yo[:, q, l, :], yp[:, l % 2, 0:C], slot_w[:, bass.ds(e * NSLOT + l, 1)],
                                            None, ALU.mult).then_inc(S["ye"], 1)

            turns(dve, NE, lambda: None, body, lambda: None)
        run.close()
        s.clear()


def moe(nc, name, xn, res, scores, w):
    with ExitStack() as stack:
        s = Scope(nc, stack, name)
        slot_tok = s.sb("slot_tok", [P, NE * NSLOT], I32)
        slot_w = s.sb("slot_w", [P, NE * NSLOT])
        choose(nc, name + "c", scores, w, slot_tok, slot_w)
        experts(nc, name + "x", xn, res, w, slot_tok, slot_w)


def attention(nc, x2, x3, xn3, scores, w):
    NH, HD = 16, 16
    HV = HD + 1
    HT = P // HD
    PAIRS = NH // 2
    GP = HT // 2
    NU = 2 * PAIRS
    with ExitStack() as stack:
        s = Scope(nc, stack, "t")
        wq = s.sb("wq", [P, KC, C])
        wk_ = s.sb("wk", [P, KC, C])
        wv = s.sb("wv", [P, KC, C])
        wp = s.sb("wp", [P, KC, C])
        bp = s.sb("bp", [P, C])
        w_g = s.sb("w_g", [P, KC, NE])
        ident = s.sb("ident", [P, P])
        causal = s.sb("causal", [P, P])
        heads = s.sb("heads", [P, HT, HV])
        half = s.sb("half", [P, 2])
        nhalf = s.sb("nhalf", [P, TJ])
        xt = s.sb("xt", [P, TJ, C])
        stat = s.sb("stat", [P, TJ, 6])
        mv = s.sb("mv", [P, TJ, 2])
        ve = s.sb("ve", [P, TJ])
        rstd = s.sb("rstd", [P, TJ])
        xn = s.sb("xn", [P, TJ, C])
        xnT = s.sb("xnT", [P, KC, T])
        neg = s.sb("neg", [P, 2, T])
        phiq = s.sb("phiq", [P, 2, KC, T])
        phim = s.sb("phim", [P, 2, 2, KC, T])
        phik = s.sb("phik", [P, 2, KC, T])
        phikt = s.sb("phikt", [P, TJ, C])
        v1 = s.sb("v1", [P, 2, TJ, NH, HV])
        state = s.sb("state", [P, TJ - 1, KC, HT * HV])
        am = s.sb("am", [P, 2, 2, 2, P])
        den = s.sb("den", [P, TJ, NH])
        rden = s.sb("rden", [P, TJ, NH])
        yt = s.sb("yt", [P, TJ, NH, HD])
        yT = s.sb("yT", [P, KC, T])
        xb = s.sb("xb", [P, 2, TJ, C])
        stat1 = s.sb("stat1", [P, TJ, 6])
        mv1 = s.sb("mv1", [P, TJ, 2])
        ve1 = s.sb("ve1", [P, TJ])
        rstd1 = s.sb("rstd1", [P, TJ])
        xn1t = s.sb("xn1t", [P, TJ, C])
        xn1T = s.sb("xn1T", [P, KC, T])
        sc = s.sb("sc", [NE, T])

        a_ps = s.ps("a_ps", [P, 2, T])
        num = s.ps("num", [P, 2, T])
        wb = s.ps("wb", [P, 2, T])
        pb = s.ps("pb", [P, T])
        kvb = s.ps("kvb", [P, T])

        loads = [(wq, w["wq"]), (wk_, w["wk"]), (wv, w["wv"]), (wp, w["wp"]), (bp, w["bp"]), (w_g, w["g_T"]),
                 (ident, w["ident"]), (causal, w["causal"]), (heads, w["heads"]), (half, w["half"])]
        S = {n: s.sem(n) for n in
             ("tick ld_w ld_x st_x3 st_xn st_sc const bs agg ve rstd xn xb tr trev qk neg ex phi msk v vev kt ktev "
              "kv st A mask av den rden y yt ytev pj x3 bs1 agg1 ve1 rstd1 xn1 pt ptev scm scev").split()}
        xv = x2.rearrange("(b j p) c -> b p j c", j=TJ, p=P)
        x3v = x3.rearrange("(b j p) c -> b p j c", j=TJ, p=P)
        xn3v = xn3.rearrange("(b j p) c -> b p j c", j=TJ, p=P)
        scv = scores.rearrange("e (b t) -> b e t", t=T)
        run = ExitStack()
        block = run.enter_context(nc.Block())

        @block.sync
        def _(sp):
            for tile, src in loads:
                sp.dma_start(tile[:], src).then_inc(S["ld_w"], 16)

            def store(b, par):
                wait_alone(sp, S["x3"], b * TJ + TJ, S["tick"])
                sp.dma_start(x3v[b], xb[:, par, :, :]).then_inc(S["st_x3"], 16)
                wait_alone(sp, S["xn1"], b + 1, S["tick"])
                sp.dma_start(xn3v[b], xn1t[:]).then_inc(S["st_xn"], 16)
                wait_alone(sp, S["scev"], b + 1, S["tick"])
                sp.dma_start(scv[b], sc[:]).then_inc(S["st_sc"], 16)

            def prologue():
                sp.dma_start(xt[:], xv[0]).then_inc(S["ld_x"], 16)

            def body(b, par, first, last):
                if not last:
                    wait_alone(sp, S["xn"], b + 1, S["tick"])
                    wait_alone(sp, S["xb"], b + 1, S["tick"])
                    sp.dma_start(xt[:], xv[b + 1]).then_inc(S["ld_x"], 16)
                else:
                    sp.wait_ge(S["xb"], NB)
                if not first:
                    store(b - 1, 1 - par)

            def epilogue():
                store(NB - 1, (NB - 1) % 2)
                for n in ("st_x3", "st_xn", "st_sc"):
                    sp.wait_ge(S[n], NB * 16)

            turns(sp, NB, prologue, body, epilogue)

        @block.gpsimd
        def _(pool):
            def inv_std(b, var, ve_, rstd_, agg, sve, srs):
                wait_alone(pool, S[agg], b + 1, S["tick"])
                nc.gpsimd.tensor_scalar(ve_[:, :], var[:, :, 1], EPS, None, ALU.add).then_inc(S[sve], 1)
                wait_alone(pool, S[sve], b + 1, S["tick"])
                nc.gpsimd.tensor_tensor(rstd_[:, :], ve_[:, :], nhalf[:, :], ALU.pow).then_inc(S[srs], 1)

            def add_bias(b, par):
                pool.wait_ge(S["ld_x"], b * 16 + 16)
                if not below(b, 2):
                    pool.wait_ge(S["st_x3"], b * 16 - 16)
                    pool.wait_ge(S["xn1"], b - 1)
                nc.gpsimd.tensor_tensor(xb[:, par, :, :], xt[:],
                                        bp[:].rearrange("p (o c) -> p o c", o=1).to_broadcast([P, TJ, C]),
                                        ALU.add).then_inc(S["xb"], 1)

            def split_heads(b, par):
                wait_alone(pool, S["phi"], b * 4 + 2, S["tick"])
                if not below(b, 2):
                    wait_alone(pool, S["A"], b * NU - NU, S["tick"])
                for r in range(2):
                    last = nc.gpsimd.tensor_scalar(phim[:, par, r, :, :], phiq[:, par, :, :], half[:, r:r + 1], 0.0,
                                                   ALU.mult, ALU.add)
                last.then_inc(S["msk"], 1)

            def prologue():
                nc.gpsimd.memset(nhalf[:], -0.5).then_inc(S["const"], 1)
                nc.gpsimd.memset(v1[:], 1.0).then_inc(S["const"], 1)
                pool.wait_ge(S["const"], 2)
                pool.wait_ge(S["ld_w"], 16 * len(loads))
                inv_std(0, mv, ve, rstd, "agg", "ve", "rstd")
                add_bias(0, 0)
                split_heads(0, 0)

            def body(b, par, first, last):
                if not last:
                    inv_std(b + 1, mv, ve, rstd, "agg", "ve", "rstd")
                if not first:
                    inv_std(b - 1, mv1, ve1, rstd1, "agg1", "ve1", "rstd1")
                if not last:
                    split_heads(b + 1, 1 - par)
                    add_bias(b + 1, 1 - par)

            turns(pool, NB, prologue, body,
                  lambda: inv_std(NB - 1, mv1, ve1, rstd1, "agg1", "ve1", "rstd1"))

        @block.scalar
        def _(act):
            def tr_out(b, k):
                act.wait_ge(S["tr"], b * 2 + k + 1)
                if k == 0 and not below(b, 1):
                    act.wait_ge(S["v"], b * 2)
                nc.scalar.copy(xnT[:, k, :], wb[:, k, :]).then_inc(S["trev"], 1)

            def exp_neg(b, m):
                act.wait_ge(S["qk"], b * 4 + m + 1)
                if not below(b * 4 + m, 2):
                    act.wait_ge(S["phi"], b * 4 + m - 1)
                nc.scalar.activation(neg[:, m % 2, :], wb[:, m % 2, :], ACT.Relu, scale=-1.0).then_inc(S["neg"], 1)
                act.wait_ge(S["neg"], b * 4 + m + 1)
                nc.scalar.activation(neg[:, m % 2, :], neg[:, m % 2, :], ACT.Exp, scale=-1.0).then_inc(S["ex"], 1)

            def v_out(b, par, m):
                act.wait_ge(S["v"], b * 2 + m + 1)
                if m == 0 and not below(b, 2):
                    act.wait_ge(S["av"], b * NU - NU)
                nc.scalar.copy(v1[:, par, 2 * m:2 * m + 2, :, 0:HD],
                               wb[:, m, :].rearrange("p (j h d) -> p j h d", j=2, d=HD)).then_inc(S["vev"], 1)

            def kt_out(b, m):
                act.wait_ge(S["kt"], b * 2 + m + 1)
                if m == 0 and not below(b, 1):
                    act.wait_ge(S["kv"], b * 3)
                nc.scalar.copy(phikt[:, 2 * m:2 * m + 2, :], wb[:, m, :].rearrange("p (j c) -> p j c", j=2))\
                    .then_inc(S["ktev"], 1)

            def yT_out(b, k):
                act.wait_ge(S["yt"], b * 2 + k + 1)
                if k == 0 and not below(b, 1):
                    act.wait_ge(S["pj"], b * TJ)
                nc.scalar.copy(yT[:, k, :], pb[:, :]).then_inc(S["ytev"], 1)

            def pt_out(b, k):
                act.wait_ge(S["pt"], b * 2 + k + 1)
                if k == 0 and not below(b, 1):
                    act.wait_ge(S["scm"], b)
                nc.scalar.copy(xn1T[:, k, :], pb[:, :]).then_inc(S["ptev"], 1)

            def sc_out(b):
                act.wait_ge(S["scm"], b + 1)
                if not below(b, 1):
                    act.wait_ge(S["st_sc"], b * 16)
                nc.scalar.copy(sc[:, :], pb[0:NE, :]).then_inc(S["scev"], 1)

            def prologue():
                for k in range(2):
                    tr_out(0, k)
                for m in range(4):
                    exp_neg(0, m)
                act.wait_ge(S["const"], 2)
                for m in range(2):
                    v_out(0, 0, m)
                for m in range(2):
                    kt_out(0, m)

            def body(b, par, first, last):
                for un in range(NU):
                    if not first:
                        if un in (2, 3):
                            yT_out(b - 1, un - 2)
                        if un in (12, 13):
                            pt_out(b - 1, un - 12)
                        if un == 14:
                            sc_out(b - 1)
                    if not last:
                        if un in (3, 4):
                            tr_out(b + 1, un - 3)
                        if 5 <= un < 9:
                            exp_neg(b + 1, un - 5)
                        if un in (9, 10):
                            v_out(b + 1, 1 - par, un - 9)
                        if un in (11, 12):
                            kt_out(b + 1, un - 11)

            def epilogue():
                for k in range(2):
                    yT_out(NB - 1, k)
                for k in range(2):
                    pt_out(NB - 1, k)
                sc_out(NB - 1)

            turns(act, NB, prologue, body, epilogue)

        @block.vector
        def _(dve):
            def in_norm1(b):
                dve.wait_ge(S["ld_x"], b * 16 + 16)
                for j in range(TJ):
                    last = nc.vector.bn_stats(stat[:, j, :], xt[:, j, :])
                last.then_inc(S["bs"], 1)
                wait_alone(dve, S["bs"], b + 1, S["tick"])
                for j in range(TJ):
                    last = nc.vector.bn_aggr(mv[:, j, :], stat[:, j, :])
                last.then_inc(S["agg"], 1)

            def in_norm2(b):
                dve.wait_ge(S["rstd"], b + 1)
                if not below(b, 1):
                    dve.wait_ge(S["tr"], b * 2)
                for j in range(TJ):
                    last = nc.vector.tensor_scalar(xn[:, j, :], xt[:, j, :], mv[:, j, 0:1], rstd[:, j:j + 1],
                                                   ALU.subtract, ALU.mult)
                last.then_inc(S["xn"], 1)

            def phi(b, par, m):
                dve.wait_ge(S["ex"], b * 4 + m + 1)
                out = (phiq if m < 2 else phik)[:, par, m % 2, :]
                if m == 0 and not below(b, 2):
                    dve.wait_ge(S["av"], b * NU - NU)
                nc.vector.scalar_tensor_tensor(out, wb[:, m % 2, :], 0.0, neg[:, m % 2, :], ALU.max, ALU.add)\
                    .then_inc(S["phi"], 1)

            def keep_state(b, j):
                dve.wait_ge(S["kv"], b * 3 + j + 1)
                if j == 0 and not below(b, 1):
                    dve.wait_ge(S["av"], b * NU)
                nc.vector.tensor_tensor(
                    state[:, j, :, :], kvb[:, 0:2 * HT * HV].rearrange("p (k n) -> p k n", k=KC),
                    heads[:].rearrange("p h v -> p (h v)").rearrange("p (o n) -> p o n", o=1)
                    .to_broadcast([P, KC, HT * HV]), ALU.mult).then_inc(S["st"], 1)

            def mask(b, un):
                g = b * NU + un
                dve.wait_ge(S["A"], g + 1)
                if not below(g, 2):
                    dve.wait_ge(S["av"], g - 1)
                nc.vector.tensor_tensor(
                    am[:, un % 2, :, :, :].rearrange("p j r c -> p (j r) c"),
                    a_ps[:, un % 2, :].rearrange("p (n c) -> p n c", c=P),
                    causal[:].rearrange("p (o c) -> p o c", o=1).to_broadcast([P, 4, P]),
                    ALU.mult).then_inc(S["mask"], 1)

            def divide(b, jp):
                dve.wait_ge(S["av"], b * NU + (jp + 1) * PAIRS)
                if not below(b, 1):
                    dve.wait_ge(S["yt"], b * 2)
                for jj in range(2):
                    nv = num[:, jj, 0:NH * HV].rearrange("p (h v) -> p h v", v=HV)
                    nc.vector.tensor_scalar(den[:, 2 * jp + jj, :], nv[:, :, HD], 1e-6, None, ALU.add)\
                        .then_inc(S["den"], 1)
                for jj in range(2):
                    dve.wait_ge(S["den"], b * 4 + 2 * jp + jj + 1)
                    nc.vector.reciprocal(rden[:, 2 * jp + jj, :], den[:, 2 * jp + jj, :]).then_inc(S["rden"], 1)
                for jj in range(2):
                    j = 2 * jp + jj
                    nv = num[:, jj, 0:NH * HV].rearrange("p (h v) -> p h v", v=HV)
                    dve.wait_ge(S["rden"], b * 4 + j + 1)
                    nc.vector.tensor_tensor(yt[:, j, :, :], nv[:, :, 0:HD],
                                            rden[:, j, :].rearrange("p (h o) -> p h o", o=1)
                                            .to_broadcast([P, NH, HD]), ALU.mult).then_inc(S["y"], 1)

            def residual(b, par, j):
                dve.wait_ge(S["pj"], b * TJ + j + 1)
                if j == 0:
                    dve.wait_ge(S["xb"], b + 1)
                nc.vector.tensor_tensor(xb[:, par, j, :], pb[:, 0:C], xb[:, par, j, :], ALU.add)\
                    .then_inc(S["x3"], 1)

            def out_norm1(b, par):
                dve.wait_ge(S["x3"], b * TJ + TJ)
                for j in range(TJ):
                    last = nc.vector.bn_stats(stat1[:, j, :], xb[:, par, j, :])
                last.then_inc(S["bs1"], 1)
                wait_alone(dve, S["bs1"], b + 1, S["tick"])
                for j in range(TJ):
                    last = nc.vector.bn_aggr(mv1[:, j, :], stat1[:, j, :])
                last.then_inc(S["agg1"], 1)

            def out_norm2(b, par):
                dve.wait_ge(S["rstd1"], b + 1)
                if not below(b, 1):
                    dve.wait_ge(S["pt"], b * 2)
                    dve.wait_ge(S["st_xn"], b * 16)
                for j in range(TJ):
                    last = nc.vector.tensor_scalar(xn1t[:, j, :], xb[:, par, j, :], mv1[:, j, 0:1],
                                                   rstd1[:, j:j + 1], ALU.subtract, ALU.mult)
                last.then_inc(S["xn1"], 1)

            def prologue():
                dve.wait_ge(S["ld_w"], 16 * len(loads))
                in_norm1(0)
                in_norm2(0)
                for m in range(4):
                    phi(0, 0, m)
                for j in range(3):
                    keep_state(0, j)

            def body(b, par, first, last):
                for un in range(NU):
                    mask(b, un)
                    if un == PAIRS:
                        divide(b, 0)
                    if not first:
                        if un == 0:
                            divide(b - 1, 1)
                        if 4 <= un < 8:
                            residual(b - 1, 1 - par, un - 4)
                        if un == 8:
                            out_norm1(b - 1, 1 - par)
                        if un == 10:
                            out_norm2(b - 1, 1 - par)
                    if not last:
                        if un == 0:
                            in_norm1(b + 1)
                        if un == 2:
                            in_norm2(b + 1)
                        if 5 <= un < 9:
                            phi(b + 1, 1 - par, un - 5)
                if not last:
                    for j in range(3):
                        keep_state(b + 1, j)

            def epilogue():
                last = (NB - 1) % 2
                divide(NB - 1, 1)
                for j in range(TJ):
                    residual(NB - 1, last, j)
                out_norm1(NB - 1, last)
                out_norm2(NB - 1, last)

            turns(dve, NB, prologue, body, epilogue)

        @block.tensor
        def _(pe):
            def mm(out, lhsT, rhs, first, last, **kw):
                return nc.tensor.matmul(out, lhsT, rhs, start=first, stop=last, **kw)

            def tr(b, k):
                pe.wait_ge(S["xn"], b + 1)
                if not below(b, 1):
                    pe.wait_ge(S["ktev"], b * 2 - 1 + k)
                for j in range(TJ):
                    last = nc.tensor.transpose(wb[:, k, j * P:(j + 1) * P], xn[:, j, k * P:(k + 1) * P], ident[:])
                last.then_inc(S["tr"], 1)

            def qk(b, m):
                pe.wait_ge(S["trev"], b * 2 + 2)
                if m >= 2:
                    pe.wait_ge(S["phi"], b * 4 + m - 1)
                wt, f = (wq, wk_)[m // 2], m % 2
                for k in range(KC):
                    last = mm(wb[:, m % 2, :], wt[:, k, f * P:(f + 1) * P], xnT[:, k, :], k == 0, k == KC - 1)
                last.then_inc(S["qk"], 1)

            def values(b, m):
                pe.wait_ge(S["phi"], b * 4 + m + 3)
                for jj in range(2):
                    j = 2 * m + jj
                    for k in range(KC):
                        last = mm(wb[:, m, jj * C:(jj + 1) * C], xnT[:, k, j * P:(j + 1) * P], wv[:, k, :],
                                  k == 0, k == KC - 1)
                last.then_inc(S["v"], 1)

            def kt(b, par, m):
                pe.wait_ge(S["vev"], b * 2 + m + 1)
                for n in range(4):
                    last = nc.tensor.transpose(wb[:, m, n * P:(n + 1) * P],
                                               phik[:, par, n % 2, (2 * m + n // 2) * P:(2 * m + n // 2 + 1) * P],
                                               ident[:])
                last.then_inc(S["kt"], 1)

            def kv(b, par, j):
                pe.wait_ge(S["ktev"], b * 2 + j // 2 + 1)
                if j:
                    pe.wait_ge(S["st"], b * 3 + j)
                elif not below(b, 1):
                    pe.wait_ge(S["st"], b * 3)
                for k in range(KC):
                    last = mm(kvb[:, k * HT * HV:(k + 1) * HT * HV], phikt[:, j, k * P:(k + 1) * P],
                              v1[:, par, j, k * HT:(k + 1) * HT, :], j == 0 and k == 0, False,
                              skip_group_check=True)
                last.then_inc(S["kv"], 1)

            def products(b, par, un):
                g = b * NU + un
                jp, pr = un // PAIRS, un % PAIRS
                f, r = pr // GP, (pr % GP) * 32
                if un == 0:
                    pe.wait_ge(S["msk"], b + 1)
                    pe.wait_ge(S["phi"], b * 4 + 4)
                if not below(g, 2):
                    pe.wait_ge(S["mask"], g - 1)
                for jj in range(2):
                    c = slice((2 * jp + jj) * P, (2 * jp + jj + 1) * P)
                    last = mm(a_ps[:, un % 2, jj * 2 * P:(jj + 1) * 2 * P], phik[r:r + 32, par, f, c],
                              phim[r:r + 32, par, :, f, c], True, True)
                last.then_inc(S["A"], 1)

            def weighted(b, par, un):
                jp, pr = un // PAIRS, un % PAIRS
                if pr == 0:
                    if jp == 1:
                        pe.wait_ge(S["y"], b * 4 + 2)
                    elif not below(b, 1):
                        pe.wait_ge(S["y"], b * 4)
                    pe.wait_ge(S["st"], b * 3 + 3)
                    for jj in range(2):
                        j = 2 * jp + jj
                        for f in range(KC if j else 0):
                            mm(num[:, jj, f * HT * HV:(f + 1) * HT * HV], phiq[:, par, f, j * P:(j + 1) * P],
                               state[:, j - 1, f, :], f == 0, False, skip_group_check=True)
                pe.wait_ge(S["mask"], b * NU + un + 1)
                for jj in range(2):
                    j = 2 * jp + jj
                    for r in range(2):
                        hd = 2 * pr + r
                        last = mm(num[:, jj, hd * HV:(hd + 1) * HV], am[:, un % 2, jj, r, :],
                                  v1[:, par, j, hd, :], j == 0 and hd == 0, False, skip_group_check=True)
                last.then_inc(S["av"], 1)

            def ytr(b, k):
                if k == 0:
                    pe.wait_ge(S["y"], b * 4 + 4)
                    if not below(b, 1):
                        pe.wait_ge(S["scev"], b)
                else:
                    pe.wait_ge(S["ytev"], b * 2 + 1)
                for j in range(TJ):
                    last = nc.tensor.transpose(
                        pb[:, j * P:(j + 1) * P],
                        yt[:, j, k * HT:(k + 1) * HT, :].rearrange("p h d -> p (h d)"), ident[:])
                last.then_inc(S["yt"], 1)

            def project(b, j):
                if j == 0:
                    pe.wait_ge(S["ytev"], b * 2 + 2)
                else:
                    pe.wait_ge(S["x3"], b * TJ + j)
                for k in range(KC):
                    last = mm(pb[:, 0:C], yT[:, k, j * P:(j + 1) * P], wp[:, k, :], k == 0, k == KC - 1)
                last.then_inc(S["pj"], 1)

            def ptr(b, k):
                if k == 0:
                    pe.wait_ge(S["xn1"], b + 1)
                else:
                    pe.wait_ge(S["ptev"], b * 2 + 1)
                for j in range(TJ):
                    last = nc.tensor.transpose(pb[:, j * P:(j + 1) * P], xn1t[:, j, k * P:(k + 1) * P], ident[:])
                last.then_inc(S["pt"], 1)

            def gate_scores(b):
                pe.wait_ge(S["ptev"], b * 2 + 2)
                for k in range(KC):
                    last = mm(pb[0:NE, :], w_g[:, k, :], xn1T[:, k, :], k == 0, k == KC - 1)
                last.then_inc(S["scm"], 1)

            def prologue():
                pe.wait_ge(S["ld_w"], 16 * len(loads))
                for k in range(2):
                    tr(0, k)
                for m in range(4):
                    qk(0, m)
                for m in range(2):
                    values(0, m)
                for m in range(2):
                    kt(0, 0, m)
                for j in range(3):
                    kv(0, 0, j)

            def body(b, par, first, last):
                for un in range(NU):
                    products(b, par, un)
                    if un:
                        weighted(b, par, un - 1)
                    if not first:
                        if un in (2, 3):
                            ytr(b - 1, un - 2)
                        if 4 <= un < 8:
                            project(b - 1, un - 4)
                        if un in (12, 13):
                            ptr(b - 1, un - 12)
                        if un == 14:
                            gate_scores(b - 1)
                    if not last:
                        if un in (3, 4):
                            tr(b + 1, un - 3)
                        if 5 <= un < 9:
                            qk(b + 1, un - 5)
                        if un in (9, 10):
                            values(b + 1, un - 9)
                        if un in (11, 12):
                            kt(b + 1, 1 - par, un - 11)
                        if un == 15:
                            kv(b + 1, 1 - par, 0)
                weighted(b, par, NU - 1)
                if not last:
                    for j in (1, 2):
                        kv(b + 1, 1 - par, j)

            def epilogue():
                for k in range(2):
                    ytr(NB - 1, k)
                for j in range(TJ):
                    project(NB - 1, j)
                for k in range(2):
                    ptr(NB - 1, k)
                gate_scores(NB - 1)

            turns(pe, NB, prologue, body, epilogue)
        run.close()
        s.clear()


def arrange(inputs):
    import numpy as np

    a = {k: np.asarray(v) for k, v in inputs.items()}
    ma = {k[len("L0_attn_a_"):]: v for k, v in a.items() if k.startswith("L0_attn_a_")}
    at = {k[len("L0_attn_b_"):]: v for k, v in a.items() if k.startswith("L0_attn_b_")}
    ff = {k[len("L0_ffn_"):]: v for k, v in a.items() if k.startswith("L0_ffn_")}

    def rows(m):
        return m.reshape(m.shape[0] // P, P, *m.shape[1:]).swapaxes(0, 1)

    xp = rows(ma["x_proj_w"].T)
    row = np.arange(P)
    bits = [1 << (30 - i) for i in range(31)] + [0]
    identity = np.eye(P, dtype=np.float32)
    pick = np.concatenate([np.eye(2 * NS, dtype=np.float32)] * 3, 0)
    out = {
        "x": ma["hidden_states"],
        "in_T": rows(ma["in_proj_w"].T),
        "xd_T": xp[:, :, 0:RK],
        "xb_T": np.concatenate([xp[:, :, RK:]] * 3, 2),
        "dt_T": ma["dt_proj_w"].T,
        "out_T": rows(ma["out_proj_w"].T),
        "g_T": rows(ff["Wg"].T),
        "conv_w": rows(ma["conv_w"]),
        "conv_b": rows(ma["conv_b"]),
        "dt_b": rows(ma["dt_proj_b"]),
        "d_par": rows(ma["D_param"]),
        "a_log": rows(ma["A_log"]),
        "ident": identity,
        "pick": pick,
        "w1": np.stack([rows(m.T) for m in ff["W1"]]),
        "w3": np.stack([rows(m.T) for m in ff["W3"]]),
        "w2": np.stack([rows(m.T) for m in ff["W2"]]),
        "blk": (row[:, None] // NB == row[None, :] // NB).astype(np.float32),
        "low": ((row[:, None] // NB == row[None, :] // NB) & (row[:, None] < row[None, :])).astype(np.float32),
        "bitf": np.tile(np.array(bits, np.float32), (P, 1)),
        "biti": np.tile(np.array(bits, np.int32), (P, 1)),
        "wq": rows(at["Wq"].T),
        "wk": rows(at["Wk"].T),
        "wv": rows(at["Wv"].T),
        "wp": rows(at["Wp"].T),
        "bp": np.tile(at["bp"], (P, 1)),
        "causal": (row[:, None] <= row[None, :]).astype(np.float32),
        "heads": np.repeat((row[:, None] // 16 == np.arange(8)[None, :]).astype(np.float32)[:, :, None], 17, 2),
        "half": (row[:, None] // 16 % 2 == np.arange(2)[None, :]).astype(np.float32),
        "part": row[:, None].astype(np.float32),
        "col": np.tile(row.astype(np.float32), (P, 1)),
    }
    return {k: np.ascontiguousarray(v) for k, v in out.items()}


def program(nc, a, out):
    x1 = nc.dram_tensor("x1", (NTOK, C), F32, kind="Internal").ap()
    xn1 = nc.dram_tensor("xn1", (NTOK, C), F32, kind="Internal").ap()
    sc1 = nc.dram_tensor("sc1", (NE, NTOK), F32, kind="Internal").ap()
    xn3 = nc.dram_tensor("xn3", (NTOK, C), F32, kind="Internal").ap()
    sc3 = nc.dram_tensor("sc3", (NE, NTOK), F32, kind="Internal").ap()
    mamba(nc, a["x"], x1, xn1, sc1, a)
    moe(nc, "f", xn1, x1, sc1, a)
    attention(nc, x1, out, xn3, sc3, a)
    moe(nc, "g", xn3, out, sc3, a)


def kernel(**inputs):
    from concourse import bacc
    from concourse.bass_utils import run_bass_kernel_spmd

    nc = bacc.Bacc("TRN2", target_bir_lowering=False, num_devices=1)
    arrays = {f"in_{name}": a for name, a in arrange(inputs).items()}
    a = {name[3:]: nc.dram_tensor(name, v.shape, mybir.dt.from_np(v.dtype), kind="ExternalInput").ap()
         for name, v in arrays.items()}
    out = nc.dram_tensor("out", (NTOK, C), F32, kind="ExternalOutput").ap()
    program(nc, a, out)
    r = run_bass_kernel_spmd(nc, [arrays], core_ids=[0])
    return r.results[0]["out"].reshape(NB, T, C)
```

```python
from contextlib import ExitStack

import concourse.bass as bass
from concourse import mybir

F32 = mybir.dt.float32
BF16 = mybir.dt.bfloat16
I32 = mybir.dt.int32
ALU = mybir.AluOpType
ACT = mybir.ActivationFunctionType
AX = mybir.AxisListType

P = 128
NB = 16
T = 512
C = 256
KC = C // P
TJ = T // P
NTOK = NB * T
EPS = 1e-5

DI = 512
KD = DI // P
NS = 16
RK = 64
CW = 4
HALO = CW - 1
UN = KD * NS

NE = 8
CAP = NTOK // NE
FH = 512
KF = FH // P
NSLOT = CAP // P


class Scope:

    def __init__(self, nc, stack, name):
        self.nc, self.stack, self.name, self.sems = nc, stack, name, []

    def sb(self, name, shape, dt=F32):
        return self.stack.enter_context(self.nc.sbuf_tensor(f"{self.name}_{name}", shape, dt))

    def ps(self, name, shape, dt=F32):
        return self.stack.enter_context(self.nc.psum_tensor(f"{self.name}_{name}", shape, dt))

    def sem(self, name):
        self.sems.append(self.stack.enter_context(self.nc.semaphore(f"{self.name}_{name}")))
        return self.sems[-1]

    def clear(self):
        with self.nc.Block() as block:
            @block.sync
            def _(sp):
                for sem in self.sems:
                    sp.sem_clear(sem)


def turns(eng, n, prologue, body, epilogue):
    prologue()
    body(0, 0, True, False)
    body(1, 1, False, False)
    with eng.Fori(1, n // 2 - 1) as k:
        for q in range(2):
            body(eng.snap(k * 2 + q), q, False, False)
    body(n - 2, 0, False, False)
    body(n - 1, 1, False, True)
    epilogue()


def mamba(nc, x, x1, xn1, scores, w):
    with ExitStack() as stack:
        s = Scope(nc, stack, "m")
        w_in = s.sb("w_in", [P, KC, 2 * DI])
        w_x = s.sb("w_x", [P, KD, RK + 2 * NS])
        w_dt = s.sb("w_dt", [RK, DI])
        w_out = s.sb("w_out", [P, KD, C])
        w_g = s.sb("w_g", [P, KC, NE])
        conv_w = s.sb("conv_w", [P, KD, CW])
        conv_b = s.sb("conv_b", [P, KD])
        dt_b = s.sb("dt_b", [P, KD])
        d_par = s.sb("d_par", [P, KD])
        a_log = s.sb("a_log", [P, KD, NS])
        a_neg = s.sb("a_neg", [P, KD, NS])
        ident = s.sb("ident", [P, P])
        pick = s.sb("pick", [6 * NS, 2 * NS])
        pickb = s.sb("pickb", [6 * NS, 2 * NS], BF16)
        nhalf = s.sb("nhalf", [P, TJ])
        xt = s.sb("xt", [P, TJ, C])
        stat = s.sb("stat", [P, TJ, 6])
        mv = s.sb("mv", [P, TJ, 2])
        ve = s.sb("ve", [P, TJ])
        rstd = s.sb("rstd", [P, TJ])
        nm = s.sb("nm", [P, TJ])
        xn = s.sb("xn", [P, TJ, C])
        xnT = s.sb("xnT", [P, KC, T])
        xs = s.sb("xs", [P, 2, HALO + T])
        dtlo = s.sb("dtlo", [RK, T])
        bc1 = s.sb("bc1", [6 * NS, T], BF16)
        bcr = s.sb("bcr", [6 * NS, T])
        bc2 = s.sb("bc2", [6 * NS, T], BF16)
        sp = s.sb("sp", [P, 2, T])
        u = s.sb("u", [P, 2, KD, T])
        sz = s.sb("sz", [P, 2, KD, T])
        delta = s.sb("delta", [P, 2, KD, T])
        du = s.sb("du", [P, 2, KD, T])
        bc = s.sb("bc", [P, 2 * NS, T])
        dbu = s.sb("dbu", [P, 4, T])
        hc = s.sb("hc", [P, 4, T])
        yg = s.sb("yg", [P, KD, T])
        xr = s.sb("xr", [P, TJ, C])
        x1t = xr
        stat1 = s.sb("stat1", [P, TJ, 6])
        mv1 = s.sb("mv1", [P, TJ, 2])
        ve1 = s.sb("ve1", [P, TJ])
        rstd1 = s.sb("rstd1", [P, TJ])
        nm1 = s.sb("nm1", [P, TJ])
        xn1t = s.sb("xn1t", [P, TJ, C])
        sc = s.sb("sc", [NE, T])

        dah = s.ps("dah", [P, 4, T])
        y = s.ps("y", [P, T])
        wk = s.ps("wk", [P, 3, T])
        ROW_BANK = (1, 0, 2)

        first_loads = [(ident, w["ident"]), (w_in, w["in_T"])]
        loads = [(conv_w, w["conv_w"]), (conv_b, w["conv_b"]), (a_log, w["a_log"]), (pick, w["pick"]),
                 (w_x, w["x_T"]), (w_dt, w["dt_T"]), (dt_b, w["dt_b"]), (d_par, w["d_par"]),
                 (w_out, w["out_T"]), (w_g, w["g_T"])]

        names = ("tick ld_w0 ld_w ld_x ld_xr st_x1 st_xn1 st_sc a_exp aneg const halo "
                 "bs agg ve rstd nm xn tr trev ix ixev cvc cv u iz izev sz xp xdev t1 xbev t2 t T dt dtev "
                 "ab ex sp de du bc bcev "
                 "dA dBu scan hC sum yt yg op x1 bs1 agg1 ve1 rstd1 nm1 xn1 pt ptev scm scev").split()
        S = {n: s.sem(n) for n in names}

        xv = x.rearrange("b (j p) c -> b p j c", p=P)
        x1v = x1.rearrange("(b j p) c -> b p j c", j=TJ, p=P)
        xn1v = xn1.rearrange("(b j p) c -> b p j c", j=TJ, p=P)
        scv = scores.rearrange("e (b t) -> b e t", t=T)

        run = ExitStack()
        block = run.enter_context(nc.Block())

        ROWS_PE, ROWS_ACT = 13, 10

        ROWS = slice(RK, RK + 2 * NS)

        def batches(eng, prologue, body, epilogue):
            turns(eng, NB, prologue, lambda b, par, first, last: body(b, par, not first, not last), epilogue)

        @block.sync
        def _(sp_):
            def load_x(b):
                sp_.dma_start(xt[:], xv[b]).then_inc(S["ld_x"], 16)

            def load_xr(b, first=False):
                if not first:
                    wait_alone(sp_, S["xn1"], b, S["tick"])
                    wait_alone(sp_, S["st_x1"], b * 16, S["tick"])
                sp_.dma_start(xr[:], xv[b]).then_inc(S["ld_xr"], 16)

            def store(b):
                wait_alone(sp_, S["x1"], b * 2 + 2, S["tick"])
                sp_.dma_start(x1v[b], x1t[:]).then_inc(S["st_x1"], 16)
                wait_alone(sp_, S["xn1"], b + 1, S["tick"])
                sp_.dma_start(xn1v[b], xn1t[:]).then_inc(S["st_xn1"], 16)
                wait_alone(sp_, S["scev"], b + 1, S["tick"])
                sp_.dma_start(scv[b], sc[:]).then_inc(S["st_sc"], 16)

            def prologue():
                load_x(0)
                for tile, src in first_loads:
                    sp_.dma_start(tile[:], src).then_inc(S["ld_w0"], 16)
                for tile, src in loads:
                    sp_.dma_start(tile[:], src).then_inc(S["ld_w"], 16)
                load_xr(0, True)

            def body(b, par, post, prep):
                if prep:
                    wait_alone(sp_, S["xn"], b + 1, S["tick"])
                    load_x(b + 1)
                if post:
                    store(b - 1)
                    load_xr(b)

            def epilogue():
                store(NB - 1)
                sp_.wait_ge(S["st_x1"], NB * 16)
                sp_.wait_ge(S["st_xn1"], NB * 16)
                sp_.wait_ge(S["st_sc"], NB * 16)
                sp_.wait_ge(S["ld_x"], NB * 16)

            batches(sp_, prologue, body, epilogue)

        @block.scalar
        def _(act):
            def scan_exp(b, par, un):
                dt, n = un // NS, un % NS
                if n == 0:
                    act.wait_ge(S["de"], b * 4 + dt + 1)
                if not (isinstance(b, int) and b * UN + un < 4):
                    act.wait_ge(S["hC"], b * UN + un - 3)
                nc.scalar.activation(dah[:, un % 4, :], delta[:, par, dt, :], ACT.Exp,
                                     scale=a_neg[:, dt, n:n + 1]).then_inc(S["dA"], 1)

            def in_norm2(b, half):
                act.wait_ge(S["nm"], b + 1)
                act.wait_ge(S["tr"], b * 2)
                for j in range(half * 2, half * 2 + 2):
                    last = nc.scalar.activation(xn[:, j, :], xt[:, j, :], ACT.Identity, bias=nm[:, j:j + 1],
                                                scale=rstd[:, j:j + 1])
                if half:
                    last.then_inc(S["xn"], 1)

            def out_norm3(b, half):
                act.wait_ge(S["nm1"], b + 1)
                if half == 0:
                    act.wait_ge(S["pt"], b * 2)
                    act.wait_ge(S["st_xn1"], b * 16)
                for j in range(half * 2, half * 2 + 2):
                    last = nc.scalar.activation(xn1t[:, j, :], x1t[:, j, :], ACT.Identity, bias=nm1[:, j:j + 1],
                                                scale=rstd1[:, j:j + 1])
                if half:
                    last.then_inc(S["xn1"], 1)

            def tr_out(b, k):
                act.wait_ge(S["tr"], b * 2 + k + 1)
                if not (isinstance(b, int) and b < 3):
                    act.wait_ge(S["scm"], b - 2)
                act.wait_ge(S["iz"], b * 4)
                nc.scalar.copy(xnT[:, k, :], wk[:, (k + 1) % 2, :]).then_inc(S["trev"], 1)

            def ix_out(b, par, dt):
                act.wait_ge(S["ix"], b * 4 + dt + 1)
                if dt >= 2 or not (isinstance(b, int) and b == 0):
                    act.wait_ge(S["cv"], b * 4 + dt - 1)
                nc.scalar.copy(xs[:, dt % 2, HALO:], wk[:, 1, :])
                nc.scalar.activation(u[:, par, dt, :], wk[:, 1, :], ACT.Identity, bias=conv_b[:, dt:dt + 1],
                                     scale=conv_w[:, dt, HALO:]).then_inc(S["ixev"], 1)

            def iz_out(b, par, dt):
                act.wait_ge(S["iz"], b * 4 + dt + 1)
                if not (isinstance(b, int) and b < 2):
                    act.wait_ge(S["yg"], b * 4 - 4)
                nc.scalar.copy(sz[:, par, dt, :], wk[:, 0, :]).then_inc(S["izev"], 1)

            def silu_u(b, par):
                act.wait_ge(S["cv"], b * 4 + 4)
                nc.scalar.activation(u[:, par, :, :], u[:, par, :, :], ACT.Silu).then_inc(S["u"], 1)
                nc.scalar.preload_act_table_set("natural_log_exp_and_others")

            def silu_z(b, par):
                act.wait_ge(S["izev"], b * 4 + 4)
                nc.scalar.activation(sz[:, par, :, :], sz[:, par, :, :], ACT.Silu).then_inc(S["sz"], 1)
                nc.scalar.preload_act_table_set("natural_log_exp_and_others")

            def xd_out(b):
                act.wait_ge(S["xp"], b + 1)
                act.wait_ge(S["dt"], b * 4)
                nc.scalar.copy(dtlo[:, :], wk[0:RK, 0, :]).then_inc(S["xdev"], 1)

            def softplus1(b, par, dt):
                act.wait_ge(S["dt"], b * 4 + dt + 1)
                if dt >= 2 or not (isinstance(b, int) and b == 0):
                    act.wait_ge(S["de"], b * 4 + dt - 1)
                v = wk[:, (dt + 1) % 2, :]
                nc.scalar.activation(sp[:, dt % 2, :], v, ACT.Abs, bias=dt_b[:, dt:dt + 1]).then_inc(S["ab"], 1)
                nc.scalar.activation(delta[:, par, dt, :], v, ACT.Relu,
                                     bias=dt_b[:, dt:dt + 1]).then_inc(S["dtev"], 1)

            def softplus2(b, dt):
                act.wait_ge(S["ab"], b * 4 + dt + 1)
                nc.scalar.activation(sp[:, dt % 2, :], sp[:, dt % 2, :], ACT.Exp, scale=-1.0).then_inc(S["ex"], 1)
                act.wait_ge(S["ex"], b * 4 + dt + 1)
                nc.scalar.activation(sp[:, dt % 2, :], sp[:, dt % 2, :], ACT.Ln, bias=1.0).then_inc(S["sp"], 1)

            def bc_out(b, j):
                act.wait_ge(S["bc"], b * 2 * NS + j + 1)
                if not (isinstance(b, int) and b == 0):
                    act.wait_ge(S["hC" if j % 2 else "dBu"], (b - 1) * UN + (KD - 1) * NS + j // 2 + 1)
                nc.scalar.copy(bc[:, j, :], wk[:, ROW_BANK[j % 3], :]).then_inc(S["bcev"], 1)

            def pt_out(b, k):
                act.wait_ge(S["pt"], b * 2 + k + 1)
                if isinstance(b, int) and b >= NB - 2:
                    act.wait_ge(S["iz"], NB * 4)
                else:
                    act.wait_ge(S["iz"], (b + 3) * 4)
                if not (isinstance(b, int) and b == 0):
                    act.wait_ge(S["scm"], b)
                nc.scalar.copy(xnT[:, k, :], wk[:, 2, :]).then_inc(S["ptev"], 1)

            def sc_out(b):
                act.wait_ge(S["scm"], b + 1)
                act.wait_ge(S["st_sc"], b * 16)
                nc.scalar.copy(sc[:, :], wk[0:NE, 2, :]).then_inc(S["scev"], 1)

            def prologue():
                nc.scalar.preload_act_table_set("natural_log_exp_and_others")
                in_norm2(0, 0)
                in_norm2(0, 1)
                for k in range(KC):
                    tr_out(0, k)
                act.wait_ge(S["ld_w"], 16 * len(loads))
                nc.scalar.activation(a_neg[:], a_log[:], ACT.Exp).then_inc(S["a_exp"], 1)
                act.wait_ge(S["a_exp"], 1)
                nc.scalar.mul(a_neg[:], a_neg[:], -1.0).then_inc(S["aneg"], 1)
                act.wait_ge(S["aneg"], 1)
                act.wait_ge(S["halo"], 1)
                for dt in range(KD):
                    ix_out(0, 0, dt)
                    iz_out(0, 0, dt)
                silu_u(0, 0)
                silu_z(0, 0)
                xd_out(0)
                for dt in range(KD):
                    softplus1(0, 0, dt)
                    softplus2(0, dt)
                for j in range(2 * ROWS_ACT):
                    bc_out(0, j)

            def body(b, par, post, prep):
                for un in range(UN):
                    scan_exp(b, par, un)
                    if un < NS - ROWS_ACT:
                        bc_out(b, 2 * (ROWS_ACT + un))
                        bc_out(b, 2 * (ROWS_ACT + un) + 1)
                    if prep and un in (7, 8):
                        in_norm2(b + 1, un - 7)
                    if post and un in (22, 23):
                        out_norm3(b - 1, un - 22)
                    if prep:
                        if un in (12, 13):
                            tr_out(b + 1, un - 12)
                        if 17 <= un < 33 and un % 4 == 1:
                            ix_out(b + 1, 1 - par, (un - 17) // 4)
                        if 17 <= un < 33 and un % 4 == 3:
                            iz_out(b + 1, 1 - par, (un - 19) // 4)
                    if post and un == 42:
                        pt_out(b - 1, 0)
                    if prep and un == 34:
                        silu_u(b + 1, 1 - par)
                    if prep and un == 38:
                        silu_z(b + 1, 1 - par)
                    if post:
                        if un == 44:
                            pt_out(b - 1, 1)
                        if un == 47:
                            sc_out(b - 1)
                    if prep:
                        if un == 41:
                            xd_out(b + 1)
                        if un in (45, 47, 49, 51):
                            softplus1(b + 1, 1 - par, (45, 47, 49, 51).index(un))
                        if un in (46, 48, 50, 52):
                            softplus2(b + 1, (46, 48, 50, 52).index(un))
                        if un >= UN - ROWS_ACT:
                            bc_out(b + 1, 2 * (un - (UN - ROWS_ACT)))
                            bc_out(b + 1, 2 * (un - (UN - ROWS_ACT)) + 1)

            def epilogue():
                out_norm3(NB - 1, 0)
                out_norm3(NB - 1, 1)
                pt_out(NB - 1, 0)
                pt_out(NB - 1, 1)
                sc_out(NB - 1)

            batches(act, prologue, body, epilogue)

        @block.gpsimd
        def _(pool):
            def inv_std(b, var, ve_, rstd_, nm_, agg, sve, srs, snm):
                wait_alone(pool, S[agg], b + 1, S["tick"])
                nc.gpsimd.tensor_scalar(ve_[:, :], var[:, :, 1], EPS, None, ALU.add).then_inc(S[sve], 1)
                nc.gpsimd.tensor_scalar(nm_[:, :], var[:, :, 0], -1.0, None, ALU.mult).then_inc(S[sve], 1)
                wait_alone(pool, S[sve], b * 2 + 2, S["tick"])
                nc.gpsimd.tensor_tensor(rstd_[:, :], ve_[:, :], nhalf[:, :], ALU.pow).then_inc(S[srs], 1)
                wait_alone(pool, S[srs], b + 1, S["tick"])
                nc.gpsimd.tensor_tensor(nm_[:, :], nm_[:, :], rstd_[:, :], ALU.mult).then_inc(S[snm], 1)

            def in_stats(b):
                inv_std(b, mv, ve, rstd, nm, "agg", "ve", "rstd", "nm")

            def out_stats(b):
                inv_std(b, mv1, ve1, rstd1, nm1, "agg1", "ve1", "rstd1", "nm1")

            def times_b(b, par, un):
                dt, n = un // NS, un % NS
                if n == 0:
                    pool.wait_ge(S["du"], b * 4 + dt + 1)
                if dt == 0:
                    pool.wait_ge(S["bcev"], b * 2 * NS + 2 * n + 1)
                if not (isinstance(b, int) and b * UN + un < 4):
                    pool.wait_ge(S["scan"], b * UN + un - 3)
                nc.gpsimd.tensor_tensor(dbu[:, un % 4, :], du[:, par, dt, :], bc[:, 2 * n, :],
                                        ALU.mult).then_inc(S["dBu"], 1)

            def mk_du(b, par, dt):
                pool.wait_ge(S["de"], b * 4 + dt + 1)
                if dt == 0:
                    pool.wait_ge(S["u"], b + 1)
                    if not (isinstance(b, int) and b < 2):
                        pool.wait_ge(S["dBu"], b * UN - UN)
                nc.gpsimd.tensor_tensor(du[:, par, dt, :], delta[:, par, dt, :], u[:, par, dt, :],
                                        ALU.mult).then_inc(S["du"], 1)

            def gate2(b, par, dt):
                if dt == 0:
                    pool.wait_ge(S["sz"], b + 1)
                pool.wait_ge(S["yt"], b * 4 + dt + 1)
                nc.gpsimd.tensor_tensor(yg[:, dt, :], yg[:, dt, :], sz[:, par, dt, :], ALU.mult).then_inc(S["yg"], 1)

            def prologue():
                nc.gpsimd.memset(nhalf[:], -0.5).then_inc(S["const"], 1)
                pool.wait_ge(S["const"], 1)
                in_stats(0)
                for dt in range(KD):
                    mk_du(0, 0, dt)

            def body(b, par, post, prep):
                for un in range(UN):
                    times_b(b, par, un)
                    if post and un == 7:
                        gate2(b - 1, 1 - par, KD - 1)
                    if un in (24, 40, 56):
                        gate2(b, par, (un - 24) // NS)
                    if post and un == 21:
                        out_stats(b - 1)
                    if prep and un in (50, 52, 55, 57):
                        mk_du(b + 1, 1 - par, (50, 52, 55, 57).index(un))
                    if prep and un == 6:
                        in_stats(b + 1)

            def epilogue():
                gate2(NB - 1, (NB - 1) % 2, KD - 1)
                out_stats(NB - 1)

            batches(pool, prologue, body, epilogue)

        @block.vector
        def _(dve):
            def in_norm1(b):
                dve.wait_ge(S["ld_x"], b * 16 + 16)
                for j in range(TJ):
                    last = nc.vector.bn_stats(stat[:, j, :], xt[:, j, :])
                last.then_inc(S["bs"], 1)
                wait_alone(dve, S["bs"], b + 1, S["tick"])
                for j in range(TJ):
                    last = nc.vector.bn_aggr(mv[:, j, :], stat[:, j, :])
                last.then_inc(S["agg"], 1)

            def conv(b, par, dt, k):
                o = u[:, par, dt, :]
                if k == 0:
                    dve.wait_ge(S["ixev"], b * 4 + dt + 1)
                else:
                    dve.wait_ge(S["cvc"], (b * 4 + dt) * 2 + k)
                nc.vector.scalar_tensor_tensor(o, xs[:, dt % 2, k:k + T], conv_w[:, dt, k:k + 1], o,
                                               ALU.mult, ALU.add).then_inc(S["cvc" if k < 2 else "cv"], 1)

            def split1(b):
                dve.wait_ge(S["xp"], b + 1)
                dve.wait_ge(S["bc"], b * 2 * NS)
                nc.vector.tensor_copy(bc1[ROWS], wk[ROWS, 0, :]).then_inc(S["t1"], 1)

            def split2(b):
                dve.wait_ge(S["t1"], b + 1)
                nc.vector.tensor_tensor(bcr[ROWS], wk[ROWS, 0, :], bc1[ROWS], ALU.subtract).then_inc(S["xbev"], 1)

            def split3(b):
                dve.wait_ge(S["xbev"], b + 1)
                nc.vector.tensor_copy(bc2[ROWS], bcr[ROWS]).then_inc(S["t2"], 1)

            def split4(b):
                dve.wait_ge(S["t2"], b + 1)
                nc.vector.tensor_tensor(bc1[0:2 * NS], bcr[ROWS], bc2[ROWS], ALU.subtract)
                nc.vector.tensor_copy(bc1[2 * NS:4 * NS], bc2[ROWS]).then_inc(S["T"], 1)

            splits = (split1, split2, split3, split4)

            def mk_delta(b, par, dt):
                dve.wait_ge(S["sp"], b * 4 + dt + 1)
                d = delta[:, par, dt, :]
                nc.vector.tensor_tensor(d, d, sp[:, dt % 2, :], ALU.add).then_inc(S["de"], 1)

            def scan(b, par, un):
                g = b * UN + un
                dve.wait_ge(S["dA"], g + 1)
                dve.wait_ge(S["dBu"], g + 1)
                nc.vector.tensor_tensor_scan(dah[:, un % 4, :], dah[:, un % 4, :], dbu[:, un % 4, :], 0.0,
                                             ALU.mult, ALU.add).then_inc(S["scan"], 1)

            def times_c(b, par, un):
                dt, n = un // NS, un % NS
                g = b * UN + un
                dve.wait_ge(S["scan"], g + 1)
                if dt == 0:
                    dve.wait_ge(S["bcev"], b * 2 * NS + 2 * n + 2)
                if not (isinstance(b, int) and b * UN + un < 4):
                    dve.wait_ge(S["sum"], g - 3)
                nc.vector.tensor_tensor(hc[:, un % 4, :], dah[:, un % 4, :], bc[:, 2 * n + 1, :],
                                        ALU.mult).then_inc(S["hC"], 1)

            def gate1(b, par, dt):
                dve.wait_ge(S["sum"], b * UN + (dt + 1) * NS)
                if dt == 0:
                    dve.wait_ge(S["u"], b + 1)
                    dve.wait_ge(S["op"], b * 4)
                nc.vector.scalar_tensor_tensor(yg[:, dt, :], u[:, par, dt, :], d_par[:, dt:dt + 1], y[:, :],
                                               ALU.mult, ALU.add).then_inc(S["yt"], 1)

            def residual(b, half):
                dve.wait_ge(S["op"], b * 4 + half * 2 + 2)
                if half == 0:
                    dve.wait_ge(S["ld_xr"], b * 16 + 16)
                two = slice(half * 2, half * 2 + 2)
                nc.vector.tensor_tensor(x1t[:, two, :], wk[:, 2, :].rearrange("p (j c) -> p j c", c=C), xr[:, two, :],
                                        ALU.add).then_inc(S["x1"], 1)

            def out_norm1(b, half):
                dve.wait_ge(S["x1"], b * 2 + half + 1)
                for j in range(half * 2, half * 2 + 2):
                    last = nc.vector.bn_stats(stat1[:, j, :], x1t[:, j, :])
                if half:
                    last.then_inc(S["bs1"], 1)

            def out_norm2(b):
                wait_alone(dve, S["bs1"], b + 1, S["tick"])
                for j in range(TJ):
                    last = nc.vector.bn_aggr(mv1[:, j, :], stat1[:, j, :])
                last.then_inc(S["agg1"], 1)

            def prologue():
                nc.vector.memset(xs[:, :, 0:HALO], 0.0).then_inc(S["halo"], 1)
                in_norm1(0)
                dve.wait_ge(S["halo"], 1)
                dve.wait_ge(S["ld_w"], 16 * len(loads))
                nc.vector.tensor_copy(pickb[:], pick[:]).then_inc(S["halo"], 1)
                for dt in range(KD):
                    for k in range(HALO):
                        conv(0, 0, dt, k)
                for split in splits:
                    split(0)
                for dt in range(KD):
                    mk_delta(0, 0, dt)

            def body(b, par, post, prep):
                for un in range(UN):
                    scan(b, par, un)
                    if un:
                        times_c(b, par, un - 1)
                    if un in (18, 34, 50):
                        gate1(b, par, (un - 18) // NS)
                    if post:
                        if un == 2:
                            gate1(b - 1, 1 - par, KD - 1)
                        if un in (10, 14):
                            residual(b - 1, (un - 10) // 4)
                        if un in (11, 15):
                            out_norm1(b - 1, (un - 11) // 4)
                        if un == 16:
                            out_norm2(b - 1)
                    if prep:
                        if un == 0:
                            in_norm1(b + 1)
                        if 16 <= un < 32 and un % 4 < HALO:
                            conv(b + 1, 1 - par, (un - 16) // 4, un % 4)
                        if 41 <= un < 45:
                            splits[un - 41](b + 1)
                        if un in (46, 48, 50, 52):
                            mk_delta(b + 1, 1 - par, (46, 48, 50, 52).index(un))
                times_c(b, par, UN - 1)

            def epilogue():
                gate1(NB - 1, (NB - 1) % 2, KD - 1)
                for half in range(2):
                    residual(NB - 1, half)
                    out_norm1(NB - 1, half)
                out_norm2(NB - 1)

            batches(dve, prologue, body, epilogue)

        @block.tensor
        def _(pe):
            def mm(out, lhsT, rhs, first, last):
                return nc.tensor.matmul(out, lhsT, rhs, start=first, stop=last)

            def tr(b, k):
                pe.wait_ge(S["xn"], b + 1)
                for j in range(TJ):
                    last = nc.tensor.transpose(wk[:, (k + 1) % 2, j * P:(j + 1) * P],
                                               xn[:, j, k * P:(k + 1) * P], ident[:])
                last.then_inc(S["tr"], 1)

            def ix(b, dt, k):
                if k == 0:
                    if dt == 0:
                        pe.wait_ge(S["trev"], b * 2 + 2)
                    else:
                        pe.wait_ge(S["ixev"], b * 4 + dt)
                one = mm(wk[:, 1, :], w_in[:, k, dt * P:(dt + 1) * P], xnT[:, k, :], k == 0, k == KC - 1)
                if k == KC - 1:
                    one.then_inc(S["ix"], 1)

            def iz(b, dt, k):
                if dt and k == 0:
                    pe.wait_ge(S["izev"], b * 4 + dt)
                one = mm(wk[:, 0, :], w_in[:, k, DI + dt * P:DI + (dt + 1) * P], xnT[:, k, :], k == 0, k == KC - 1)
                if k == KC - 1:
                    one.then_inc(S["iz"], 1)

            def xp(b, par, k):
                if k == 0:
                    pe.wait_ge(S["u"], b + 1)
                    pe.wait_ge(S["izev"], b * 4 + 4)
                one = mm(wk[0:RK + 2 * NS, 0, :], w_x[:, k, :], u[:, par, k, :], k == 0, k == KD - 1)
                if k == KD - 1:
                    one.then_inc(S["xp"], 1)

            def dtp(b, dt):
                if dt == 0:
                    pe.wait_ge(S["xdev"], b + 1)
                elif dt == 1:
                    pe.wait_ge(S["xbev"], b + 1)
                else:
                    pe.wait_ge(S["dtev"], b * 4 + dt - 1)
                mm(wk[:, (dt + 1) % 2, :], w_dt[:, dt * P:(dt + 1) * P], dtlo[:, :], True, True)\
                    .then_inc(S["dt"], 1)

            def bcast(b, j, post=True):
                if j == 0:
                    pe.wait_ge(S["T"], b + 1)
                if j < 2:
                    pe.wait_ge(S["dtev"], b * 4 + j + 3)
                elif j > 2:
                    pe.wait_ge(S["bcev"], b * 2 * NS + j - 2)
                elif post:
                    pe.wait_ge(S["scev"], b - 1)
                row = j // 2 + (NS if j % 2 else 0)
                mm(wk[:, ROW_BANK[j % 3], :], pickb[:, row:row + 1].to_broadcast([96, P]), bc1[:], True, True)\
                    .then_inc(S["bc"], 1)

            def total(b, un):
                dt, n = un // NS, un % NS
                g = b * UN + un
                if n == 0 and not (isinstance(b, int) and b == 0 and dt < 1):
                    pe.wait_ge(S["yt"], b * 4 + dt)
                pe.wait_ge(S["hC"], g + 1)
                mm(y[:, :], ident[:], hc[:, un % 4, :], n == 0, n == NS - 1).then_inc(S["sum"], 1)

            def outp(b, j, ending=False):
                if j == 0:
                    pe.wait_ge(S["yg"], b * 4 + 4)
                    if ending:
                        pe.wait_ge(S["scev"], NB - 1)
                    else:
                        pe.wait_ge(S["bcev"], (b + 2) * 2 * NS)
                elif j == 2:
                    pe.wait_ge(S["x1"], b * 2 + 1)
                for k in range(KD):
                    last = mm(wk[:, 2, (j % 2) * C:(j % 2 + 1) * C], yg[:, k, j * P:(j + 1) * P], w_out[:, k, :],
                              k == 0, k == KD - 1)
                last.then_inc(S["op"], 1)

            def ptr(b, k):
                if k == 0:
                    pe.wait_ge(S["xn1"], b + 1)
                else:
                    pe.wait_ge(S["ptev"], b * 2 + 1)
                for j in range(TJ):
                    last = nc.tensor.transpose(wk[:, 2, j * P:(j + 1) * P], xn1t[:, j, k * P:(k + 1) * P], ident[:])
                last.then_inc(S["pt"], 1)

            def gate_scores(b):
                pe.wait_ge(S["ptev"], b * 2 + 2)
                for k in range(KC):
                    last = mm(wk[0:NE, 2, :], w_g[:, k, :], xnT[:, k, :], k == 0, k == KC - 1)
                last.then_inc(S["scm"], 1)

            def prologue():
                pe.wait_ge(S["ld_w0"], 16 * len(first_loads))
                for k in range(KC):
                    tr(0, k)
                for dt in range(KD):
                    for k in range(KC):
                        ix(0, dt, k)
                    for k in range(KC):
                        iz(0, dt, k)
                pe.wait_ge(S["ld_w"], 16 * len(loads))
                for k in range(KD):
                    xp(0, 0, k)
                for dt in range(KD):
                    dtp(0, dt)
                for j in range(2 * ROWS_PE):
                    bcast(0, j, False)

            def body(b, par, post, prep):
                for un in range(UN):
                    if un >= 2:
                        total(b, un - 2)
                    elif post:
                        total(b - 1, UN - 2 + un)
                    if un < NS - ROWS_PE:
                        bcast(b, 2 * (ROWS_PE + un))
                        bcast(b, 2 * (ROWS_PE + un) + 1)
                    if post:
                        if un in (6, 7):
                            outp(b - 1, un - 6)
                        if un in (10, 11):
                            outp(b - 1, un - 8)
                        if un == 38:
                            ptr(b - 1, 0)
                        if un == 40:
                            ptr(b - 1, 1)
                        if un == 42:
                            gate_scores(b - 1)
                    if prep:
                        if un == 7 and not post:
                            pe.wait_ge(S["bcev"], 2 * NS)
                        if un in (8, 9):
                            tr(b + 1, un - 8)
                        if 12 <= un < 28:
                            (ix, iz)[un // 2 % 2](b + 1, (un - 12) // 4, un % 2)
                        if 34 <= un < 38:
                            xp(b + 1, 1 - par, un - 34)
                        if un in (41, 43, 45, 47):
                            dtp(b + 1, (41, 43, 45, 47).index(un))
                        if un >= UN - ROWS_PE:
                            bcast(b + 1, 2 * (un - (UN - ROWS_PE)), post)
                            bcast(b + 1, 2 * (un - (UN - ROWS_PE)) + 1, post)
                if not prep:
                    total(b, UN - 2)
                    total(b, UN - 1)

            def epilogue():
                for j in range(TJ):
                    outp(NB - 1, j, True)
                for k in range(KC):
                    ptr(NB - 1, k)
                gate_scores(NB - 1)

            batches(pe, prologue, body, epilogue)
        run.close()
        s.clear()


def below(i, n):
    return isinstance(i, int) and i < n


def wait_alone(eng, sem, value, tick):
    eng.wait_ge(sem, value)
    eng.sem_inc(tick, 1)


def choose(nc, name, scores, w, slot_tok, slot_w, xn, tok, xg, gathered):
    PAIR = 3
    ROUNDS = 15
    TURN = 5
    with ExitStack() as keep:
        k = Scope(nc, keep, name)
        lo = k.sb("lo", [P, T], BF16)
        hi = k.sb("hi", [P, T], BF16)
        wp = k.sb("wp", [P, 3, T], BF16)
        with ExitStack() as stack:
            s = Scope(nc, stack, name + "a")
            sc = s.sb("sc", [P, T])
            blk = s.sb("blk", [P, P])
            low = s.sb("low", [P, P])
            ident = s.sb("ident", [P, P])
            unit = s.sb("unit", [P, 1 + ROUNDS])
            step = s.sb("step", [P, 1 + (ROUNDS + 1) * PAIR], I32)
            one = s.sb("one", [P, T])
            junk = s.sb("junk", [P, PAIR, T])
            rmax = s.sb("rmax", [P, 1])
            emax = s.sb("emax", [1, NE])
            emax_b = s.sb("emax_b", [1, NE, NB])
            nmax = s.sb("nmax", [P, 1])
            cnt = s.sb("cnt", [P, PAIR])
            enough = s.sb("enough", [P, PAIR])
            num = s.sb("num", [P, 1])
            hit = s.sb("hit", [P, 1], I32)
            found = s.sb("found", [P, 1], I32)
            trial = s.sb("trial", [P, PAIR], I32)
            gt = s.sb("gt", [P, T])
            eq = s.sb("eq", [P, T])
            cg = s.sb("cg", [P, 1])
            ce = s.sb("ce", [P, 1])
            need = s.sb("need", [P, 1])
            offe = s.sb("offe", [P, 1])
            pe_ = s.sb("pe", [P, T])
            sele = s.sb("sele", [P, T])
            sel = s.sb("sel", [P, T])
            rows = s.sb("rows", [P, 1])
            offs = s.sb("offs", [P, 1])
            ps_ = s.sb("ps", [P, T])
            pos = s.sb("pos", [P, T])
            ex = s.sb("ex", [P, T])
            ew = s.sb("ew", [P, T])
            sw = s.sb("sw", [P, 1])
            rw = s.sb("rw", [P, 1])
            wgt = s.sb("wgt", [P, T])
            posi = s.sb("posi", [P, T], I32)
            loi = s.sb("loi", [P, T], I32)
            hii = s.sb("hii", [P, T], I32)
            wr = s.sb("wr", [P, T])
            tot = s.ps("tot", [P, 512])
            mrow = s.ps("mrow", [P, 512])
            mcol = s.ps("mcol", [P, 512])
            offp = s.ps("offp", [P, 512])
            tpos = s.ps("tpos", [P, T])
            twgt = s.ps("twgt", [P, T])
            S = {n: s.sem(n) for n in
                 "ld one rmax mrow emax emb mcol nmax cnt tot num hit trial found masks offp small pe sele sel offs "
                 "ps pos ex ew sw rw wgt tp tw posi loi hii w1 wr w2 wr2 done".split()}
            consts = [(blk, w["blk"]), (low, w["low"]), (ident, w["ident"]), (unit, w["unit"]), (step, w["step"])]
            run = ExitStack()
            block = run.enter_context(nc.Block())

            @block.sync
            def _(sp):
                sp.dma_start(sc[:], scores.rearrange("e (b t) -> (e b) t", t=T)).then_inc(S["ld"], 16)
                for tile, src in consts:
                    sp.dma_start(tile[:], src).then_inc(S["ld"], 16)

            loaded = 16 * (1 + len(consts))

            @block.scalar
            def _(act):
                act.wait_ge(S["nmax"], 1)
                nc.scalar.activation(ex[:], sc[:], ACT.Exp, bias=nmax[:, 0:1]).then_inc(S["ex"], 1)

            @block.tensor
            def _(pe):
                pe.wait_ge(S["rmax"], 1)
                nc.tensor.transpose(mrow[0:1, 0:P], rmax[:], ident[:]).then_inc(S["mrow"], 1)
                pe.wait_ge(S["emb"], 1)
                nc.tensor.matmul(mcol[:, 0:1], emax_b[:, :, :].rearrange("p e b -> p (e b)"), one[0:1, 0:1],
                                 start=True, stop=True).then_inc(S["mcol"], 1)

                def total_of(r, n):
                    pe.wait_ge(S["cnt"], r + 1)
                    nc.tensor.matmul(tot[:, 0:n], blk[:], cnt[:, 0:n], start=True, stop=True).then_inc(S["tot"], 1)

                total_of(0, 1)
                total_of(1, 1)
                with pe.Fori(0, ROUNDS // TURN) as i:
                    for q in range(TURN):
                        total_of(pe.snap(i * TURN + (q + 2)), PAIR)
                pe.wait_ge(S["masks"], 2)
                nc.tensor.matmul(tot[:, 0:1], blk[:], cg[:], start=True, stop=True).then_inc(S["tot"], 1)
                nc.tensor.matmul(offp[:, 0:1], low[:], ce[:], start=True, stop=True).then_inc(S["offp"], 1)
                pe.wait_ge(S["sel"], 1)
                nc.tensor.matmul(mcol[:, 0:1], low[:], rows[:], start=True, stop=True).then_inc(S["offs"], 1)
                pe.wait_ge(S["ew"], 1)
                nc.tensor.matmul(mrow[:, 0:1], blk[:], sw[:], start=True, stop=True).then_inc(S["sw"], 1)
                pe.wait_ge(S["pos"], 1)
                for j in range(TJ):
                    last = nc.tensor.transpose(tpos[:, j * P:(j + 1) * P], pos[:, j * P:(j + 1) * P], ident[:])
                last.then_inc(S["tp"], 1)
                pe.wait_ge(S["wgt"], 1)
                for j in range(TJ):
                    last = nc.tensor.transpose(twgt[:, j * P:(j + 1) * P], wgt[:, j * P:(j + 1) * P], ident[:])
                last.then_inc(S["tw"], 1)

            @block.vector
            def _(dve):
                V = nc.vector
                V.memset(one[:], 1.0).then_inc(S["one"], 1)
                dve.wait_ge(S["one"], 1)
                dve.wait_ge(S["ld"], loaded)
                V.tensor_reduce(rmax[:], sc[:], AX.X, ALU.max).then_inc(S["rmax"], 1)
                dve.wait_ge(S["mrow"], 1)
                V.tensor_reduce(emax[:], mrow[0:1, 0:P].rearrange("p (e b) -> p e b", b=NB), AX.X, ALU.max)\
                    .then_inc(S["emax"], 1)
                dve.wait_ge(S["emax"], 1)
                V.tensor_copy(emax_b[:], emax[:].rearrange("p (e o) -> p e o", o=1).to_broadcast([1, NE, NB]))\
                    .then_inc(S["emb"], 1)
                dve.wait_ge(S["mcol"], 1)
                V.tensor_scalar(nmax[:], mcol[:, 0:1], -1.0, None, ALU.mult).then_inc(S["nmax"], 1)

                V.tensor_scalar(junk[:, 0, :], sc[:], 0.0, None, ALU.is_ge, ALU.add, accum_out=cnt[:, 0:1])\
                    .then_inc(S["cnt"], 1)
                dve.wait_ge(S["tot"], 1)
                V.tensor_scalar(found[:], tot[:, 0:1], float(CAP), -1.0, ALU.is_ge, ALU.add)\
                    .then_inc(S["found"], 1)
                dve.wait_ge(S["found"], 1)
                V.tensor_tensor(trial[:, 0:1], found[:], step[:, 0:1], ALU.bitwise_xor).then_inc(S["trial"], 1)
                dve.wait_ge(S["trial"], 1)
                V.tensor_scalar(junk[:, 0, :], sc[:], trial[:, 0:1].bitcast(F32), None, ALU.is_ge, ALU.add,
                                accum_out=cnt[:, 0:1]).then_inc(S["cnt"], 1)
                dve.wait_ge(S["tot"], 2)
                V.tensor_scalar(hit[:], tot[:, 0:1], float(CAP), unit[:, 0:1], ALU.is_ge, ALU.mult)\
                    .then_inc(S["hit"], 1)

                def next_trials(hits, steps):
                    dve.wait_ge(S["hit"], hits)
                    V.scalar_tensor_tensor(trial[:], steps, hit[:, 0:1], found[:].to_broadcast([P, PAIR]),
                                           ALU.bitwise_xor, ALU.bitwise_xor).then_inc(S["trial"], 1)

                def keep_bits():
                    V.tensor_tensor(found[:], hit[:], found[:], ALU.bitwise_xor).then_inc(S["found"], 1)

                next_trials(1, step[:, 1:1 + PAIR])
                with dve.Fori(0, ROUNDS // TURN) as i:
                    for q in range(TURN):
                        r = dve.snap(i * TURN + q)
                        dve.wait_ge(S["trial"], r + 2)
                        for v in range(PAIR):
                            last = V.tensor_scalar(junk[:, v, :], sc[:], trial[:, v:v + 1].bitcast(F32), None, ALU.is_ge,
                                                   ALU.add, accum_out=cnt[:, v:v + 1])
                            if v == 0:
                                keep_bits()
                        last.then_inc(S["cnt"], 1)
                        dve.wait_ge(S["tot"], r + 3)
                        V.tensor_scalar(enough[:], tot[:, 0:PAIR], float(CAP), None, ALU.is_ge, ALU.add,
                                        accum_out=num[:]).then_inc(S["num"], 1)
                        dve.wait_ge(S["num"], r + 1)
                        dve.wait_ge(S["found"], r + 2)
                        V.tensor_scalar(hit[:], num[:], unit[:, bass.ds(r + 1, 1)], None, ALU.mult)\
                            .then_inc(S["hit"], 1)
                        next_trials(r + 2, step[:, bass.ds(r * PAIR + (1 + PAIR), PAIR)])
                dve.wait_ge(S["trial"], ROUNDS + 2)
                keep_bits()
                dve.wait_ge(S["found"], ROUNDS + 2)
                thr = found[:].bitcast(F32)
                V.tensor_scalar(gt[:], sc[:], thr, None, ALU.is_gt, ALU.add, accum_out=cg[:]).then_inc(S["masks"], 1)
                V.tensor_scalar(eq[:], sc[:], thr, None, ALU.is_equal, ALU.add, accum_out=ce[:]).then_inc(S["masks"], 1)
                dve.wait_ge(S["tot"], ROUNDS + 3)
                V.tensor_scalar(need[:], tot[:, 0:1], -1.0, float(CAP), ALU.mult, ALU.add).then_inc(S["small"], 1)
                dve.wait_ge(S["offp"], 1)
                V.tensor_copy(offe[:], offp[:, 0:1]).then_inc(S["small"], 1)
                dve.wait_ge(S["small"], 2)
                dve.wait_ge(S["masks"], 2)
                V.tensor_tensor_scan(pe_[:], one[:], eq[:], offe[:, 0:1], ALU.mult, ALU.add).then_inc(S["pe"], 1)
                dve.wait_ge(S["pe"], 1)
                V.scalar_tensor_tensor(sele[:], pe_[:], need[:, 0:1], eq[:], ALU.is_le, ALU.mult)\
                    .then_inc(S["sele"], 1)
                dve.wait_ge(S["sele"], 1)
                V.scalar_tensor_tensor(sel[:], sele[:], 1.0, gt[:], ALU.mult, ALU.add, accum_out=rows[:])\
                    .then_inc(S["sel"], 1)
                dve.wait_ge(S["sel"], 1)
                dve.wait_ge(S["ex"], 1)
                V.scalar_tensor_tensor(ew[:], ex[:], 1.0, sel[:], ALU.mult, ALU.mult, accum_out=sw[:])\
                    .then_inc(S["ew"], 1)
                dve.wait_ge(S["offs"], 1)
                V.tensor_copy(offs[:], mcol[:, 0:1]).then_inc(S["small"], 1)
                dve.wait_ge(S["small"], 3)
                V.tensor_tensor_scan(ps_[:], one[:], sel[:], offs[:, 0:1], ALU.mult, ALU.add).then_inc(S["ps"], 1)
                dve.wait_ge(S["ps"], 1)
                V.tensor_tensor(pos[:], ps_[:], sel[:], ALU.mult).then_inc(S["pos"], 1)
                dve.wait_ge(S["sw"], 1)
                V.reciprocal(rw[:], mrow[:, 0:1]).then_inc(S["rw"], 1)
                dve.wait_ge(S["rw"], 1)
                dve.wait_ge(S["ew"], 1)
                V.tensor_scalar(wgt[:], ew[:], rw[:, 0:1], None, ALU.mult).then_inc(S["wgt"], 1)
                dve.wait_ge(S["tp"], 1)
                V.tensor_scalar(posi[:], tpos[:], -1.0, None, ALU.add).then_inc(S["posi"], 1)
                dve.wait_ge(S["posi"], 1)
                V.tensor_scalar(loi[:], posi[:], 7, None, ALU.arith_shift_right).then_inc(S["loi"], 1)
                V.tensor_scalar(hii[:], posi[:], P - 1, None, ALU.bitwise_and).then_inc(S["hii"], 1)
                dve.wait_ge(S["loi"], 1)
                V.tensor_copy(lo[:], loi[:]).then_inc(S["done"], 1)
                dve.wait_ge(S["hii"], 1)
                V.tensor_copy(hi[:], hii[:]).then_inc(S["done"], 1)
                dve.wait_ge(S["tw"], 1)
                V.tensor_copy(wp[:, 0, :], twgt[:]).then_inc(S["w1"], 1)
                dve.wait_ge(S["w1"], 1)
                V.tensor_tensor(wr[:], twgt[:], wp[:, 0, :], ALU.subtract).then_inc(S["wr"], 1)
                dve.wait_ge(S["wr"], 1)
                V.tensor_copy(wp[:, 1, :], wr[:]).then_inc(S["w2"], 1)
                dve.wait_ge(S["w2"], 1)
                V.tensor_tensor(wp[:, 2, :], wr[:], wp[:, 1, :], ALU.subtract).then_inc(S["done"], 1)
            run.close()
            s.clear()

        with ExitStack() as stack:
            s = Scope(nc, stack, name + "b")
            NV = 5
            hot = s.sb("hot", [P, P, T], BF16)
            lhot = s.sb("lhot", [P, NSLOT, T], BF16)
            val = s.sb("val", [P, NV, NSLOT, T], BF16)
            part = s.sb("part", [P, 1])
            tilei = s.sb("tilei", [P, TJ, NE, NB], I32)
            tileb = s.sb("tileb", [P, T], BF16)
            col = s.sb("col", [P, P])
            got = s.sb("got", [P, NE, NV, NSLOT])
            tokf = s.sb("tokf", [P, NE, NSLOT])
            w12 = s.sb("w12", [P, NE, NSLOT])
            acc0 = s.ps("acc0", [P, 512])
            acc = s.ps("acc", [P, 512])
            place = [(acc0 if e == 0 else acc)[:, e * NV * NSLOT:(e + 1) * NV * NSLOT] for e in range(NE)]
            S = {n: s.sem(n) for n in "tick ld iota tile lhot val hot acc got tokf w12 out tok".split()}
            run = ExitStack()
            block = run.enter_context(nc.Block())

            @block.sync
            def _(sp):
                sp.dma_start(part[:], w["part"]).then_inc(S["ld"], 16)
                sp.dma_start(col[:], w["col"]).then_inc(S["ld"], 16)

            @block.gpsimd
            def _(pool):
                nc.gpsimd.iota(tilei[:], pattern=[[1, TJ], [0, NE], [TJ, NB]], base=0, channel_multiplier=0)\
                    .then_inc(S["iota"], 1)
                pool.wait_ge(S["iota"], 1)
                nc.gpsimd.tensor_copy(tileb[:], tilei[:].rearrange("p j e b -> p (j e b)")).then_inc(S["tile"], 1)
                pool.wait_ge(S["out"], 1)
                nc.gpsimd.tensor_copy(tok[:, 0, :], slot_tok[:, 0:NSLOT]).then_inc(S["tok"], 1)
                wait_alone(pool, S["tok"], 1, S["tick"])
                for l in range(NSLOT):
                    nc.gpsimd.indirect_dma_start(
                        xg[:, 0, l, :], None, xn, bass.IndirectOffsetOnAxis(tok[:, 0, l:l + 1], 0),
                    ).then_inc(gathered, 16)

            @block.vector
            def _(dve):
                V = nc.vector
                dve.wait_ge(S["ld"], 32)
                for l in range(NSLOT):
                    V.tensor_scalar(lhot[:, l, :], lo[:], float(l), None, ALU.is_equal).then_inc(S["lhot"], 1)
                with dve.Fori(0, P // 8) as i:
                    for q in range(8):
                        V.tensor_scalar(hot[:, bass.ds(i * 8 + q, 1), :].rearrange("p o t -> p (o t)"), hi[:],
                                        col[:, bass.ds(i * 8 + q, 1)], None, ALU.is_equal).then_inc(S["hot"], 1)
                dve.wait_ge(S["lhot"], NSLOT)
                V.tensor_scalar(val[:, 0, :, :], lhot[:], part[:, 0:1], None, ALU.mult).then_inc(S["val"], 1)
                dve.wait_ge(S["tile"], 1)
                for v, src in ((1, tileb[:]), (2, wp[:, 0, :]), (3, wp[:, 1, :]), (4, wp[:, 2, :])):
                    V.tensor_tensor(val[:, v, :, :], lhot[:],
                                    src.rearrange("p (o t) -> p o t", o=1).to_broadcast([P, NSLOT, T]),
                                    ALU.mult).then_inc(S["val"], 1)
                for i, (e0, e1) in enumerate(((0, 1), (1, NE))):
                    es, slots = slice(e0, e1), slice(e0 * NSLOT, e1 * NSLOT)
                    dve.wait_ge(S["acc"], e1)
                    V.tensor_copy(got[:, es], (acc0, acc)[i][:, e0 * NV * NSLOT:e1 * NV * NSLOT]
                                  .rearrange("p (e v l) -> p e v l", v=NV, l=NSLOT)).then_inc(S["got"], 1)
                    dve.wait_ge(S["got"], i + 1)
                    V.tensor_scalar(tokf[:, es, :], got[:, es, 1, :], float(P), None, ALU.mult).then_inc(S["tokf"], 1)
                    V.tensor_tensor(w12[:, es, :], got[:, es, 2, :], got[:, es, 3, :], ALU.add).then_inc(S["w12"], 1)
                    dve.wait_ge(S["tokf"], i + 1)
                    V.tensor_tensor(slot_tok[:, slots].rearrange("p (e l) -> p e l", l=NSLOT), tokf[:, es, :],
                                    got[:, es, 0, :], ALU.add).then_inc(S["out"], 1)
                    dve.wait_ge(S["w12"], i + 1)
                    V.tensor_tensor(slot_w[:, slots].rearrange("p (e l) -> p e l", l=NSLOT), w12[:, es, :],
                                    got[:, es, 4, :], ALU.add).then_inc(S["out"], 1)

            @block.tensor
            def _(pe):
                pe.wait_ge(S["hot"], P)
                pe.wait_ge(S["val"], NV)
                for e in range(NE):
                    for n in range(NB * TJ):
                        c = (n % TJ) * P + e * NB + n // TJ
                        last = nc.tensor.matmul(place[e].rearrange("p (v l) -> p v l", l=NSLOT), hot[:, :, c], val[:, :, :, c],
                                                start=n == 0, stop=n == NB * TJ - 1)
                    last.then_inc(S["acc"], 1)
            run.close()
            s.clear()


def experts(nc, name, xn, res, w, slot_tok, slot_w, tok, xg, gathered):
    with ExitStack() as stack:
        s = Scope(nc, stack, name)
        w1 = s.sb("w1", [P, 2, KC, FH])
        w3 = s.sb("w3", [P, 2, KC, FH])
        w2 = s.sb("w2", [P, 2, KF, C])
        ident = s.sb("ident", [P, P])
        xgT = s.sb("xgT", [P, 2, KC, CAP])
        sg = s.sb("sg", [P, 2, T])
        hT = s.sb("hT", [P, 2, KF, T])
        yo = s.sb("yo", [P, 2, NSLOT, C])
        tp = s.ps("tp", [P, 2, T])
        h1 = s.ps("h1", [P, 2, T])
        h3 = s.ps("h3", [P, 2, T])
        yp = s.ps("yp", [P, 2, T])
        S = {n: s.sem(n) for n in "tick ld_id ld0 ld1 tok g1 tr xev h sg mul y ye sc".split()}
        S["g0"] = gathered
        run = ExitStack()
        block = run.enter_context(nc.Block())
        HALVES = CAP // T
        NH_ = HALVES * KF

        @block.sync
        def _(sp):
            def body(e, q, first, last):
                if not below(e, 2):
                    sp.wait_ge(S["y"], (e - 1) * NSLOT)
                sp.dma_start(w1[:, q, :, :], w["w1"][e]).then_inc(S[f"ld{q}"], 16)
                sp.dma_start(w3[:, q, :, :], w["w3"][e]).then_inc(S[f"ld{q}"], 16)
                sp.dma_start(w2[:, q, :, :], w["w2"][e]).then_inc(S[f"ld{q}"], 16)

            def prologue():
                sp.dma_start(ident[:], w["ident"]).then_inc(S["ld_id"], 16)

            turns(sp, NE, prologue, body, lambda: None)

        def loads_by(e, q):
            return 48 * (e // 2 + 1) if isinstance(e, int) else (e - q) * 24 + 48

        def gathers_by(e, q):
            return 16 * NSLOT * (e // 2 + 1) if isinstance(e, int) else (e - q) * (8 * NSLOT) + 16 * NSLOT

        @block.gpsimd
        def _(pool):
            def gather(e, q):
                if not below(e, 2):
                    pool.wait_ge(S["tr"], (e - 1) * 4)
                    pool.wait_ge(S["sc"], (e - 1) * 16 * NSLOT)
                nc.gpsimd.tensor_copy(tok[:, q, :], slot_tok[:, bass.ds(e * NSLOT, NSLOT)]).then_inc(S["tok"], 1)
                wait_alone(pool, S["tok"], e, S["tick"])
                for l in range(NSLOT):
                    nc.gpsimd.indirect_dma_start(
                        xg[:, q, l, :], None, xn, bass.IndirectOffsetOnAxis(tok[:, q, l:l + 1], 0),
                    ).then_inc(S[f"g{q}"], 16)

            def scatter(e, q):
                if not below(e, 1):
                    pool.wait_ge(S["sc"], e * 16 * NSLOT)
                for l in range(NSLOT):
                    wait_alone(pool, S["ye"], e * NSLOT + l + 1, S["tick"])
                    nc.gpsimd.indirect_dma_start(
                        res, bass.IndirectOffsetOnAxis(tok[:, q, l:l + 1], 0), yo[:, q, l, :], None,
                        compute_op=ALU.add).then_inc(S["sc"], 16)

            def body(e, q, first, last):
                if not first:
                    gather(e, q)
                    scatter(e - 1, 1 - q)

            def epilogue():
                scatter(NE - 1, (NE - 1) % 2)
                pool.wait_ge(S["sc"], NE * 16 * NSLOT)

            turns(pool, NE, lambda: None, body, epilogue)

        @block.tensor
        def _(pe):
            def transposes(e, q):
                pe.wait_ge(S[f"g{q}"], gathers_by(e, q))
                for g in range(4):
                    k, half = g % 2, g // 2
                    if not below(e * 4 + g, 2):
                        pe.wait_ge(S["xev"], e * 4 + g - 1)
                    for j in range(TJ):
                        last = nc.tensor.transpose(tp[:, g % 2, j * P:(j + 1) * P],
                                                   xg[:, q, half * TJ + j, k * P:(k + 1) * P], ident[:])
                    last.then_inc(S["tr"], 1)

            def hidden(e, q):
                pe.wait_ge(S[f"ld{q}"], loads_by(e, q))
                pe.wait_ge(S["xev"], e * 4 + 4)
                for m in range(NH_):
                    half, f = m // KF, m % KF
                    if not below(e * NH_ + m, 2):
                        pe.wait_ge(S["mul"], e * NH_ + m - 1)
                    for wt, out in ((w1, h1), (w3, h3)):
                        for k in range(KC):
                            last = nc.tensor.matmul(out[:, m % 2, :], wt[:, q, k, f * P:(f + 1) * P],
                                                    xgT[:, q, k, half * T:(half + 1) * T],
                                                    start=k == 0, stop=k == KC - 1)
                    last.then_inc(S["h"], 1)

            def outputs(e, q):
                for l in range(NSLOT):
                    half, j = l // TJ, l % TJ
                    if j == 0:
                        pe.wait_ge(S["mul"], e * NH_ + (half + 1) * KF)
                    if not below(e * NSLOT + l, 2):
                        pe.wait_ge(S["ye"], e * NSLOT + l - 1)
                    for f in range(KF):
                        last = nc.tensor.matmul(yp[:, l % 2, 0:C], hT[:, half, f, j * P:(j + 1) * P],
                                                w2[:, q, f, :], start=f == 0, stop=f == KF - 1)
                    last.then_inc(S["y"], 1)

            def prologue():
                pe.wait_ge(S["ld_id"], 16)
                transposes(0, 0)

            def body(e, q, first, last):
                hidden(e, q)
                if not last:
                    transposes(e + 1, 1 - q)
                outputs(e, q)

            turns(pe, NE, prologue, body, lambda: None)

        @block.scalar
        def _(act):
            def tokens_out(e, q):
                for g in range(4):
                    k, half = g % 2, g // 2
                    act.wait_ge(S["tr"], e * 4 + g + 1)
                    if g == 0 and not below(e, 2):
                        act.wait_ge(S["h"], (e - 1) * NH_)
                    nc.scalar.copy(xgT[:, q, k, half * T:(half + 1) * T], tp[:, g % 2, :]).then_inc(S["xev"], 1)

            def silus(e, q):
                for m in range(NH_):
                    act.wait_ge(S["h"], e * NH_ + m + 1)
                    if not below(e * NH_ + m, 2):
                        act.wait_ge(S["mul"], e * NH_ + m - 1)
                    nc.scalar.activation(sg[:, m % 2, :], h1[:, m % 2, :], ACT.Silu).then_inc(S["sg"], 1)

            def body(e, q, first, last):
                silus(e, q)
                if not last:
                    tokens_out(e + 1, 1 - q)

            turns(act, NE, lambda: tokens_out(0, 0), body, lambda: None)

        @block.vector
        def _(dve):
            def body(e, q, first, last):
                for m in range(NH_):
                    half, f = m // KF, m % KF
                    dve.wait_ge(S["sg"], e * NH_ + m + 1)
                    if f == 0 and not first:
                        dve.wait_ge(S["y"], e * NSLOT + half * TJ + TJ - NSLOT)
                    nc.vector.tensor_tensor(hT[:, half, f, :], sg[:, m % 2, :], h3[:, m % 2, :], ALU.mult)\
                        .then_inc(S["mul"], 1)
                for l in range(NSLOT):
                    dve.wait_ge(S["y"], e * NSLOT + l + 1)
                    if l == 0 and not below(e, 2):
                        dve.wait_ge(S["sc"], (e - 1) * 16 * NSLOT)
                    nc.vector.tensor_scalar(yo[:, q, l, :], yp[:, l % 2, 0:C], slot_w[:, bass.ds(e * NSLOT + l, 1)],
                                            None, ALU.mult).then_inc(S["ye"], 1)

            turns(dve, NE, lambda: None, body, lambda: None)
        run.close()
        s.clear()


def moe(nc, name, xn, res, scores, w):
    with ExitStack() as stack:
        s = Scope(nc, stack, name)
        slot_tok = s.sb("slot_tok", [P, NE * NSLOT], I32)
        slot_w = s.sb("slot_w", [P, NE * NSLOT])
        tok = s.sb("tok", [P, 2, NSLOT], I32)
        xg = s.sb("xg", [P, 2, NSLOT, C])
        gathered = s.sem("gathered")
        choose(nc, name + "c", scores, w, slot_tok, slot_w, xn, tok, xg, gathered)
        experts(nc, name + "x", xn, res, w, slot_tok, slot_w, tok, xg, gathered)
        s.clear()


def attention(nc, x2, x3, xn3, scores, w):
    NH, HD = 16, 16
    HV = HD + 1
    HT = P // HD
    PAIRS = NH // 2
    GP = HT // 2
    NU = 2 * PAIRS
    with ExitStack() as stack:
        s = Scope(nc, stack, "t")
        wq = s.sb("wq", [P, KC, C])
        wk_ = s.sb("wk", [P, KC, C])
        wv = s.sb("wv", [P, KC, C])
        wp = s.sb("wp", [P, KC, C])
        bp = s.sb("bp", [P, C])
        w_g = s.sb("w_g", [P, KC, NE])
        ident = s.sb("ident", [P, P])
        causal = s.sb("causal", [P, P])
        heads = s.sb("heads", [P, HT, HV])
        nhalf = s.sb("nhalf", [P, TJ])
        xt = s.sb("xt", [P, TJ, C])
        stat = s.sb("stat", [P, TJ, 6])
        mv = s.sb("mv", [P, TJ, 2])
        ve = s.sb("ve", [P, TJ])
        rstd = s.sb("rstd", [P, TJ])
        xn = s.sb("xn", [P, TJ, C])
        xnT = s.sb("xnT", [P, KC, T])
        neg = s.sb("neg", [P, 2, T])
        phiq = s.sb("phiq", [P, 2, KC, T])
        phim = s.sb("phim", [P, 2, HT, KC, T])
        phik = s.sb("phik", [P, 2, KC, T])
        phikt = s.sb("phikt", [P, TJ, C])
        v1 = s.sb("v1", [P, 2, TJ, NH, HV])
        state = s.sb("state", [P, TJ - 1, KC, HT * HV])
        am = s.sb("am", [P, 2, 2, 2, P])
        den = s.sb("den", [P, TJ, NH])
        rden = s.sb("rden", [P, TJ, NH])
        yt = s.sb("yt", [P, TJ, NH, HD])
        yT = s.sb("yT", [P, KC, T])
        xb = s.sb("xb", [P, 2, TJ, C])
        stat1 = s.sb("stat1", [P, TJ, 6])
        mv1 = s.sb("mv1", [P, TJ, 2])
        ve1 = s.sb("ve1", [P, TJ])
        rstd1 = s.sb("rstd1", [P, TJ])
        xn1t = s.sb("xn1t", [P, TJ, C])
        xn1T = s.sb("xn1T", [P, KC, T])
        sc = s.sb("sc", [NE, T])

        a_ps = s.ps("a_ps", [P, 2, T])
        num = s.ps("num", [P, 2, T])
        wb = s.ps("wb", [P, 2, T])
        pb = s.ps("pb", [P, T])
        kvb = s.ps("kvb", [P, T])

        loads = [(wq, w["wq"]), (wk_, w["wk"]), (wv, w["wv"]), (wp, w["wp"]), (bp, w["bp"]), (w_g, w["g_T"]),
                 (causal, w["causal"]), (heads, w["heads"])]
        S = {n: s.sem(n) for n in
             ("tick ld_id ld_w ld_x st_x3 st_xn st_sc const bs agg ve rstd xn xb tr trev qk neg ex phi msk v vev kt ktev "
              "kv st A mask av den rden y yt ytev pj x3 bs1 agg1 ve1 rstd1 xn1 pt ptev scm scev").split()}
        xv = x2.rearrange("(b j p) c -> b p j c", j=TJ, p=P)
        x3v = x3.rearrange("(b j p) c -> b p j c", j=TJ, p=P)
        xn3v = xn3.rearrange("(b j p) c -> b p j c", j=TJ, p=P)
        scv = scores.rearrange("e (b t) -> b e t", t=T)
        run = ExitStack()
        block = run.enter_context(nc.Block())

        @block.sync
        def _(sp):
            def store(b, par):
                wait_alone(sp, S["x3"], b * TJ + TJ, S["tick"])
                sp.dma_start(x3v[b], xb[:, par, :, :]).then_inc(S["st_x3"], 16)
                wait_alone(sp, S["xn1"], b + 1, S["tick"])
                sp.dma_start(xn3v[b], xn1t[:]).then_inc(S["st_xn"], 16)
                wait_alone(sp, S["scev"], b + 1, S["tick"])
                sp.dma_start(scv[b], sc[:]).then_inc(S["st_sc"], 16)

            def prologue():
                sp.dma_start(xt[:], xv[0]).then_inc(S["ld_x"], 16)
                sp.dma_start(ident[:], w["ident"]).then_inc(S["ld_id"], 16)
                for tile, src in loads:
                    sp.dma_start(tile[:], src).then_inc(S["ld_w"], 16)

            def body(b, par, first, last):
                if not last:
                    wait_alone(sp, S["xn"], b + 1, S["tick"])
                    wait_alone(sp, S["xb"], b + 1, S["tick"])
                    sp.dma_start(xt[:], xv[b + 1]).then_inc(S["ld_x"], 16)
                else:
                    sp.wait_ge(S["xb"], NB)
                if not first:
                    store(b - 1, 1 - par)

            def epilogue():
                store(NB - 1, (NB - 1) % 2)
                for n in ("st_x3", "st_xn", "st_sc"):
                    sp.wait_ge(S[n], NB * 16)

            turns(sp, NB, prologue, body, epilogue)

        @block.gpsimd
        def _(pool):
            def inv_std(b, var, ve_, rstd_, agg, sve, srs):
                wait_alone(pool, S[agg], b + 1, S["tick"])
                nc.gpsimd.tensor_scalar(ve_[:, :], var[:, :, 1], EPS, None, ALU.add).then_inc(S[sve], 1)
                wait_alone(pool, S[sve], b + 1, S["tick"])
                nc.gpsimd.tensor_tensor(rstd_[:, :], ve_[:, :], nhalf[:, :], ALU.pow).then_inc(S[srs], 1)

            def add_bias(b, par):
                pool.wait_ge(S["ld_x"], b * 16 + 16)
                if not below(b, 2):
                    pool.wait_ge(S["st_x3"], b * 16 - 16)
                    pool.wait_ge(S["xn1"], b - 1)
                nc.gpsimd.tensor_tensor(xb[:, par, :, :], xt[:],
                                        bp[:].rearrange("p (o c) -> p o c", o=1).to_broadcast([P, TJ, C]),
                                        ALU.add).then_inc(S["xb"], 1)

            def split_heads(b, par):
                wait_alone(pool, S["phi"], b * 4 + 2, S["tick"])
                if not below(b, 2):
                    wait_alone(pool, S["A"], b * NU - NU, S["tick"])
                for r in range(HT):
                    last = nc.gpsimd.tensor_scalar(phim[:, par, r, :, :], phiq[:, par, :, :], heads[:, r, 0:1], 0.0,
                                                   ALU.mult, ALU.add)
                last.then_inc(S["msk"], 1)

            def prologue():
                nc.gpsimd.memset(nhalf[:], -0.5).then_inc(S["const"], 1)
                nc.gpsimd.memset(v1[:], 1.0).then_inc(S["const"], 1)
                pool.wait_ge(S["const"], 2)
                inv_std(0, mv, ve, rstd, "agg", "ve", "rstd")
                pool.wait_ge(S["ld_w"], 16 * len(loads))
                add_bias(0, 0)
                split_heads(0, 0)

            def body(b, par, first, last):
                if not last:
                    inv_std(b + 1, mv, ve, rstd, "agg", "ve", "rstd")
                if not first:
                    inv_std(b - 1, mv1, ve1, rstd1, "agg1", "ve1", "rstd1")
                if not last:
                    split_heads(b + 1, 1 - par)
                    add_bias(b + 1, 1 - par)

            turns(pool, NB, prologue, body,
                  lambda: inv_std(NB - 1, mv1, ve1, rstd1, "agg1", "ve1", "rstd1"))

        @block.scalar
        def _(act):
            def tr_out(b, k):
                act.wait_ge(S["tr"], b * 2 + k + 1)
                if k == 0 and not below(b, 1):
                    act.wait_ge(S["v"], b * 2)
                nc.scalar.copy(xnT[:, k, :], wb[:, k, :]).then_inc(S["trev"], 1)

            def exp_neg(b, m):
                act.wait_ge(S["qk"], b * 4 + m + 1)
                if not below(b * 4 + m, 2):
                    act.wait_ge(S["phi"], b * 4 + m - 1)
                nc.scalar.activation(neg[:, m % 2, :], wb[:, m % 2, :], ACT.Relu, scale=-1.0).then_inc(S["neg"], 1)
                act.wait_ge(S["neg"], b * 4 + m + 1)
                nc.scalar.activation(neg[:, m % 2, :], neg[:, m % 2, :], ACT.Exp, scale=-1.0).then_inc(S["ex"], 1)

            def v_out(b, par, m):
                act.wait_ge(S["v"], b * 2 + m + 1)
                if m == 0 and not below(b, 2):
                    act.wait_ge(S["av"], b * NU - NU)
                nc.scalar.copy(v1[:, par, 2 * m:2 * m + 2, :, 0:HD],
                               wb[:, m, :].rearrange("p (j h d) -> p j h d", j=2, d=HD)).then_inc(S["vev"], 1)

            def kt_out(b, m):
                act.wait_ge(S["kt"], b * 2 + m + 1)
                if m == 0 and not below(b, 1):
                    act.wait_ge(S["kv"], b * 3)
                nc.scalar.copy(phikt[:, 2 * m:2 * m + 2, :], wb[:, m, :].rearrange("p (j c) -> p j c", j=2))\
                    .then_inc(S["ktev"], 1)

            def yT_out(b, k):
                act.wait_ge(S["yt"], b * 2 + k + 1)
                if k == 0 and not below(b, 1):
                    act.wait_ge(S["pj"], b * TJ)
                nc.scalar.copy(yT[:, k, :], pb[:, :]).then_inc(S["ytev"], 1)

            def pt_out(b, k):
                act.wait_ge(S["pt"], b * 2 + k + 1)
                if k == 0 and not below(b, 1):
                    act.wait_ge(S["scm"], b)
                nc.scalar.copy(xn1T[:, k, :], pb[:, :]).then_inc(S["ptev"], 1)

            def sc_out(b):
                act.wait_ge(S["scm"], b + 1)
                if not below(b, 1):
                    act.wait_ge(S["st_sc"], b * 16)
                nc.scalar.copy(sc[:, :], pb[0:NE, :]).then_inc(S["scev"], 1)

            def prologue():
                for k in range(2):
                    tr_out(0, k)
                for m in range(4):
                    exp_neg(0, m)
                act.wait_ge(S["const"], 2)
                for m in range(2):
                    v_out(0, 0, m)
                for m in range(2):
                    kt_out(0, m)

            def body(b, par, first, last):
                for un in range(NU):
                    if not first:
                        if un in (2, 3):
                            yT_out(b - 1, un - 2)
                        if un in (11, 13):
                            pt_out(b - 1, (un - 11) // 2)
                        if un == 15:
                            sc_out(b - 1)
                    if not last:
                        if un == 3:
                            tr_out(b + 1, 0)
                            tr_out(b + 1, 1)
                        if 4 <= un < 8:
                            exp_neg(b + 1, un - 4)
                        if un in (8, 9):
                            v_out(b + 1, 1 - par, un - 8)
                        if un in (10, 12):
                            kt_out(b + 1, (un - 10) // 2)

            def epilogue():
                for k in range(2):
                    yT_out(NB - 1, k)
                for k in range(2):
                    pt_out(NB - 1, k)
                sc_out(NB - 1)

            turns(act, NB, prologue, body, epilogue)

        @block.vector
        def _(dve):
            def in_norm1(b):
                dve.wait_ge(S["ld_x"], b * 16 + 16)
                for j in range(TJ):
                    last = nc.vector.bn_stats(stat[:, j, :], xt[:, j, :])
                last.then_inc(S["bs"], 1)
                wait_alone(dve, S["bs"], b + 1, S["tick"])
                for j in range(TJ):
                    last = nc.vector.bn_aggr(mv[:, j, :], stat[:, j, :])
                last.then_inc(S["agg"], 1)

            def in_norm2(b):
                dve.wait_ge(S["rstd"], b + 1)
                if not below(b, 1):
                    dve.wait_ge(S["tr"], b * 2)
                for j in range(TJ):
                    last = nc.vector.tensor_scalar(xn[:, j, :], xt[:, j, :], mv[:, j, 0:1], rstd[:, j:j + 1],
                                                   ALU.subtract, ALU.mult)
                last.then_inc(S["xn"], 1)

            def phi(b, par, m):
                dve.wait_ge(S["ex"], b * 4 + m + 1)
                out = (phiq if m < 2 else phik)[:, par, m % 2, :]
                if m == 0 and not below(b, 2):
                    dve.wait_ge(S["av"], b * NU - NU)
                nc.vector.scalar_tensor_tensor(out, wb[:, m % 2, :], 0.0, neg[:, m % 2, :], ALU.max, ALU.add)\
                    .then_inc(S["phi"], 1)

            def keep_state(b, j):
                dve.wait_ge(S["kv"], b * 3 + j + 1)
                if j < 2 and not below(b, 1):
                    dve.wait_ge(S["av"], (b - 1) * NU + (1, PAIRS + 1)[j])
                nc.vector.tensor_tensor(
                    state[:, j, :, :], kvb[:, 0:2 * HT * HV].rearrange("p (k n) -> p k n", k=KC),
                    heads[:].rearrange("p h v -> p (h v)").rearrange("p (o n) -> p o n", o=1)
                    .to_broadcast([P, KC, HT * HV]), ALU.mult).then_inc(S["st"], 1)

            def mask(b, un):
                g = b * NU + un
                dve.wait_ge(S["A"], g + 1)
                if not below(g, 2):
                    dve.wait_ge(S["av"], g - 1)
                nc.vector.tensor_tensor(
                    am[:, un % 2, :, :, :].rearrange("p j r c -> p (j r) c"),
                    a_ps[:, un % 2, :].rearrange("p (n c) -> p n c", c=P),
                    causal[:].rearrange("p (o c) -> p o c", o=1).to_broadcast([P, 4, P]),
                    ALU.mult).then_inc(S["mask"], 1)

            def divide(b, jp):
                dve.wait_ge(S["av"], b * NU + (jp + 1) * PAIRS)
                if not below(b, 1):
                    dve.wait_ge(S["yt"], b * 2)
                for jj in range(2):
                    nv = num[:, jj, 0:NH * HV].rearrange("p (h v) -> p h v", v=HV)
                    nc.vector.tensor_scalar(den[:, 2 * jp + jj, :], nv[:, :, HD], 1e-6, None, ALU.add)\
                        .then_inc(S["den"], 1)
                for jj in range(2):
                    dve.wait_ge(S["den"], b * 4 + 2 * jp + jj + 1)
                    nc.vector.reciprocal(rden[:, 2 * jp + jj, :], den[:, 2 * jp + jj, :]).then_inc(S["rden"], 1)
                for jj in range(2):
                    j = 2 * jp + jj
                    nv = num[:, jj, 0:NH * HV].rearrange("p (h v) -> p h v", v=HV)
                    dve.wait_ge(S["rden"], b * 4 + j + 1)
                    nc.vector.tensor_tensor(yt[:, j, :, :], nv[:, :, 0:HD],
                                            rden[:, j, :].rearrange("p (h o) -> p h o", o=1)
                                            .to_broadcast([P, NH, HD]), ALU.mult).then_inc(S["y"], 1)

            def residual(b, par, j):
                dve.wait_ge(S["pj"], b * TJ + j + 1)
                if j == 0:
                    dve.wait_ge(S["xb"], b + 1)
                nc.vector.tensor_tensor(xb[:, par, j, :], pb[:, 0:C], xb[:, par, j, :], ALU.add)\
                    .then_inc(S["x3"], 1)

            def out_norm1(b, par):
                dve.wait_ge(S["x3"], b * TJ + TJ)
                for j in range(TJ):
                    last = nc.vector.bn_stats(stat1[:, j, :], xb[:, par, j, :])
                last.then_inc(S["bs1"], 1)
                wait_alone(dve, S["bs1"], b + 1, S["tick"])
                for j in range(TJ):
                    last = nc.vector.bn_aggr(mv1[:, j, :], stat1[:, j, :])
                last.then_inc(S["agg1"], 1)

            def out_norm2(b, par):
                dve.wait_ge(S["rstd1"], b + 1)
                if not below(b, 1):
                    dve.wait_ge(S["pt"], b * 2)
                    dve.wait_ge(S["st_xn"], b * 16)
                for j in range(TJ):
                    last = nc.vector.tensor_scalar(xn1t[:, j, :], xb[:, par, j, :], mv1[:, j, 0:1],
                                                   rstd1[:, j:j + 1], ALU.subtract, ALU.mult)
                last.then_inc(S["xn1"], 1)

            def prologue():
                in_norm1(0)
                in_norm2(0)
                dve.wait_ge(S["ld_w"], 16 * len(loads))
                for m in range(4):
                    phi(0, 0, m)
                keep_state(0, 0)

            def body(b, par, first, last):
                for un in range(NU):
                    if un == PAIRS:
                        divide(b, 0)
                    if un == 0 and not first:
                        divide(b - 1, 1)
                    mask(b, un)
                    if un < 2:
                        keep_state(b, un + 1)
                    if not last:
                        if un == 0:
                            in_norm1(b + 1)
                        if un == 1:
                            in_norm2(b + 1)
                        if 5 <= un < 9:
                            phi(b + 1, 1 - par, un - 5)
                        if un == 15:
                            keep_state(b + 1, 0)
                    if not first:
                        if 4 <= un < 8:
                            residual(b - 1, 1 - par, un - 4)
                        if un == 8:
                            out_norm1(b - 1, 1 - par)
                        if un == 9:
                            out_norm2(b - 1, 1 - par)

            def epilogue():
                last = (NB - 1) % 2
                divide(NB - 1, 1)
                for j in range(TJ):
                    residual(NB - 1, last, j)
                out_norm1(NB - 1, last)
                out_norm2(NB - 1, last)

            turns(dve, NB, prologue, body, epilogue)

        @block.tensor
        def _(pe):
            def mm(out, lhsT, rhs, first, last, **kw):
                return nc.tensor.matmul(out, lhsT, rhs, start=first, stop=last, **kw)

            def tr(b, k):
                pe.wait_ge(S["xn"], b + 1)
                if not below(b, 1):
                    pe.wait_ge(S["ktev"], b * 2 - 1 + k)
                for j in range(TJ):
                    last = nc.tensor.transpose(wb[:, k, j * P:(j + 1) * P], xn[:, j, k * P:(k + 1) * P], ident[:])
                last.then_inc(S["tr"], 1)

            def qk(b, m):
                pe.wait_ge(S["trev"], b * 2 + 2)
                if m >= 2:
                    pe.wait_ge(S["phi"], b * 4 + m - 1)
                wt, f = (wq, wk_)[m // 2], m % 2
                for k in range(KC):
                    last = mm(wb[:, m % 2, :], wt[:, k, f * P:(f + 1) * P], xnT[:, k, :], k == 0, k == KC - 1)
                last.then_inc(S["qk"], 1)

            def values(b, m):
                pe.wait_ge(S["phi"], b * 4 + m + 3)
                for jj in range(2):
                    j = 2 * m + jj
                    for k in range(KC):
                        last = mm(wb[:, m, jj * C:(jj + 1) * C], xnT[:, k, j * P:(j + 1) * P], wv[:, k, :],
                                  k == 0, k == KC - 1)
                last.then_inc(S["v"], 1)

            def kt(b, par, m):
                pe.wait_ge(S["vev"], b * 2 + m + 1)
                for n in range(4):
                    last = nc.tensor.transpose(wb[:, m, n * P:(n + 1) * P],
                                               phik[:, par, n % 2, (2 * m + n // 2) * P:(2 * m + n // 2 + 1) * P],
                                               ident[:])
                last.then_inc(S["kt"], 1)

            def kv(b, par, j):
                pe.wait_ge(S["ktev"], b * 2 + j // 2 + 1)
                if j:
                    pe.wait_ge(S["st"], b * 3 + j)
                elif not below(b, 1):
                    pe.wait_ge(S["st"], b * 3)
                for k in range(KC):
                    last = mm(kvb[:, k * HT * HV:(k + 1) * HT * HV], phikt[:, j, k * P:(k + 1) * P],
                              v1[:, par, j, k * HT:(k + 1) * HT, :], j == 0 and k == 0, False,
                              skip_group_check=True)
                last.then_inc(S["kv"], 1)

            def products(b, par, un):
                g = b * NU + un
                jp, pr = un // PAIRS, un % PAIRS
                f, r = pr // GP, (pr % GP) * 2
                if un == 0:
                    pe.wait_ge(S["msk"], b + 1)
                    pe.wait_ge(S["phi"], b * 4 + 4)
                if not below(g, 2):
                    pe.wait_ge(S["mask"], g - 1)
                for jj in range(2):
                    c = slice((2 * jp + jj) * P, (2 * jp + jj + 1) * P)
                    last = mm(a_ps[:, un % 2, jj * 2 * P:(jj + 1) * 2 * P], phik[:, par, f, c],
                              phim[:, par, r:r + 2, f, c], True, True)
                last.then_inc(S["A"], 1)

            def weighted(b, par, un):
                jp, pr = un // PAIRS, un % PAIRS
                if pr == 0:
                    if jp == 1:
                        pe.wait_ge(S["y"], b * 4 + 2)
                    elif not below(b, 1):
                        pe.wait_ge(S["y"], b * 4)
                    pe.wait_ge(S["st"], b * 3 + (1, 3)[jp])
                    for jj in range(2):
                        j = 2 * jp + jj
                        for f in range(KC if j else 0):
                            mm(num[:, jj, f * HT * HV:(f + 1) * HT * HV], phiq[:, par, f, j * P:(j + 1) * P],
                               state[:, j - 1, f, :], f == 0, False, skip_group_check=True)
                pe.wait_ge(S["mask"], b * NU + un + 1)
                for jj in range(2):
                    j = 2 * jp + jj
                    for r in range(2):
                        hd = 2 * pr + r
                        last = mm(num[:, jj, hd * HV:(hd + 1) * HV], am[:, un % 2, jj, r, :],
                                  v1[:, par, j, hd, :], j == 0 and hd == 0, False, skip_group_check=True)
                last.then_inc(S["av"], 1)

            def ytr(b, k):
                if k == 0:
                    pe.wait_ge(S["y"], b * 4 + 4)
                    if not below(b, 1):
                        pe.wait_ge(S["scev"], b)
                else:
                    pe.wait_ge(S["ytev"], b * 2 + 1)
                for j in range(TJ):
                    last = nc.tensor.transpose(
                        pb[:, j * P:(j + 1) * P],
                        yt[:, j, k * HT:(k + 1) * HT, :].rearrange("p h d -> p (h d)"), ident[:])
                last.then_inc(S["yt"], 1)

            def project(b, j):
                if j == 0:
                    pe.wait_ge(S["ytev"], b * 2 + 2)
                else:
                    pe.wait_ge(S["x3"], b * TJ + j)
                for k in range(KC):
                    last = mm(pb[:, 0:C], yT[:, k, j * P:(j + 1) * P], wp[:, k, :], k == 0, k == KC - 1)
                last.then_inc(S["pj"], 1)

            def ptr(b, k):
                if k == 0:
                    pe.wait_ge(S["xn1"], b + 1)
                else:
                    pe.wait_ge(S["ptev"], b * 2 + 1)
                for j in range(TJ):
                    last = nc.tensor.transpose(pb[:, j * P:(j + 1) * P], xn1t[:, j, k * P:(k + 1) * P], ident[:])
                last.then_inc(S["pt"], 1)

            def gate_scores(b):
                pe.wait_ge(S["ptev"], b * 2 + 2)
                for k in range(KC):
                    last = mm(pb[0:NE, :], w_g[:, k, :], xn1T[:, k, :], k == 0, k == KC - 1)
                last.then_inc(S["scm"], 1)

            def prologue():
                pe.wait_ge(S["ld_id"], 16)
                for k in range(2):
                    tr(0, k)
                pe.wait_ge(S["ld_w"], 16 * len(loads))
                for m in range(4):
                    qk(0, m)
                for m in range(2):
                    values(0, m)
                for m in range(2):
                    kt(0, 0, m)
                kv(0, 0, 0)

            def body(b, par, first, last):
                for un in range(NU):
                    if un == PAIRS:
                        weighted(b, par, un - 1)
                    if un == 0 and not first:
                        weighted(b - 1, 1 - par, NU - 1)
                    products(b, par, un)
                    if un < 2:
                        kv(b, par, un + 1)
                    if not first:
                        if un in (2, 3):
                            ytr(b - 1, un - 2)
                        if 4 <= un < 8:
                            project(b - 1, un - 4)
                        if un in (11, 13):
                            ptr(b - 1, (un - 11) // 2)
                        if un == 15:
                            gate_scores(b - 1)
                    if not last:
                        if un == 3:
                            tr(b + 1, 0)
                            tr(b + 1, 1)
                        if 4 <= un < 8:
                            qk(b + 1, un - 4)
                        if un in (8, 9):
                            values(b + 1, un - 8)
                        if un in (10, 12):
                            kt(b + 1, 1 - par, (un - 10) // 2)
                        if un == 14:
                            kv(b + 1, 1 - par, 0)
                    if un not in (0, PAIRS):
                        weighted(b, par, un - 1)

            def epilogue():
                weighted(NB - 1, (NB - 1) % 2, NU - 1)
                for k in range(2):
                    ytr(NB - 1, k)
                for j in range(TJ):
                    project(NB - 1, j)
                for k in range(2):
                    ptr(NB - 1, k)
                gate_scores(NB - 1)

            turns(pe, NB, prologue, body, epilogue)
        run.close()
        s.clear()


def arrange(inputs):
    import numpy as np

    a = {k: np.asarray(v) for k, v in inputs.items()}
    ma = {k[len("L0_attn_a_"):]: v for k, v in a.items() if k.startswith("L0_attn_a_")}
    at = {k[len("L0_attn_b_"):]: v for k, v in a.items() if k.startswith("L0_attn_b_")}
    ff = {k[len("L0_ffn_"):]: v for k, v in a.items() if k.startswith("L0_ffn_")}

    def rows(m):
        return m.reshape(m.shape[0] // P, P, *m.shape[1:]).swapaxes(0, 1)

    xp = rows(ma["x_proj_w"].T)
    row = np.arange(P)
    pairs = range(28, -1, -2)
    identity = np.eye(P, dtype=np.float32)
    pick = np.concatenate([np.eye(2 * NS, dtype=np.float32)] * 3, 0)
    out = {
        "x": ma["hidden_states"],
        "in_T": rows(ma["in_proj_w"].T),
        "x_T": xp,
        "dt_T": ma["dt_proj_w"].T,
        "out_T": rows(ma["out_proj_w"].T),
        "g_T": rows(ff["Wg"].T),
        "conv_w": rows(ma["conv_w"]),
        "conv_b": rows(ma["conv_b"]),
        "dt_b": rows(ma["dt_proj_b"]),
        "d_par": rows(ma["D_param"]),
        "a_log": rows(ma["A_log"]),
        "ident": identity,
        "pick": pick,
        "w1": np.stack([rows(m.T) for m in ff["W1"]]),
        "w3": np.stack([rows(m.T) for m in ff["W3"]]),
        "w2": np.stack([rows(m.T) for m in ff["W2"]]),
        "blk": (row[:, None] // NB == row[None, :] // NB).astype(np.float32),
        "low": ((row[:, None] // NB == row[None, :] // NB) & (row[:, None] < row[None, :])).astype(np.float32),
        "unit": np.tile(np.array([1 << k for k in (30, *pairs)], np.float32), (P, 1)),
        "step": np.tile(np.array([1 << 30] + [v << k for k in pairs for v in (1, 2, 3)] + [0] * 3, np.int32), (P, 1)),
        "wq": rows(at["Wq"].T),
        "wk": rows(at["Wk"].T),
        "wv": rows(at["Wv"].T),
        "wp": rows(at["Wp"].T),
        "bp": np.tile(at["bp"], (P, 1)),
        "causal": (row[:, None] <= row[None, :]).astype(np.float32),
        "heads": np.repeat((row[:, None] // 16 == np.arange(8)[None, :]).astype(np.float32)[:, :, None], 17, 2),
        "part": row[:, None].astype(np.float32),
        "col": np.tile(row.astype(np.float32), (P, 1)),
    }
    return {k: np.ascontiguousarray(v) for k, v in out.items()}


def program(nc, a, out):
    x1 = nc.dram_tensor("x1", (NTOK, C), F32, kind="Internal").ap()
    xn1 = nc.dram_tensor("xn1", (NTOK, C), F32, kind="Internal").ap()
    sc1 = nc.dram_tensor("sc1", (NE, NTOK), F32, kind="Internal").ap()
    xn3 = nc.dram_tensor("xn3", (NTOK, C), F32, kind="Internal").ap()
    sc3 = nc.dram_tensor("sc3", (NE, NTOK), F32, kind="Internal").ap()
    mamba(nc, a["x"], x1, xn1, sc1, a)
    moe(nc, "f", xn1, x1, sc1, a)
    attention(nc, x1, out, xn3, sc3, a)
    moe(nc, "g", xn3, out, sc3, a)


def kernel(**inputs):
    from concourse import bacc
    from concourse.bass_utils import run_bass_kernel_spmd

    nc = bacc.Bacc("TRN2", target_bir_lowering=False, num_devices=1)
    arrays = {f"in_{name}": a for name, a in arrange(inputs).items()}
    a = {name[3:]: nc.dram_tensor(name, v.shape, mybir.dt.from_np(v.dtype), kind="ExternalInput").ap()
         for name, v in arrays.items()}
    out = nc.dram_tensor("out", (NTOK, C), F32, kind="ExternalOutput").ap()
    program(nc, a, out)
    r = run_bass_kernel_spmd(nc, [arrays], core_ids=[0])
    return r.results[0]["out"].reshape(NB, T, C)
```
